# Optimizing a Trainium2 kernel written in Bass

```python
import numpy as np
import jax
import jax.numpy as jnp

def _softmax(x, axis=-1):
    return jax.nn.softmax(x, axis=axis)

def _gelu(x):
    return jax.nn.gelu(x, approximate=True)

def _silu(x):
    return jax.nn.silu(x)

def _sigmoid(x):
    return jax.nn.sigmoid(x)

def _layernorm(x, axis=-1, eps=1e-05):
    m = jnp.mean(x, axis=axis, keepdims=True)
    v = jnp.var(x, axis=axis, keepdims=True)
    return (x - m) / jnp.sqrt(v + eps)

def _scatter_add(tgt, idx, src, axis=0):
    return tgt.at[idx].add(src)

def _segment_sum(src, seg, n):
    return jax.ops.segment_sum(src, seg, n)
kernel_name = 'mk_adj_seq_d1_adj_r2_2232e3'

def setup_inputs(seed: int=0):
    np.random.seed(seed)
    _w = jnp.asarray

    def _rec_inputs():
        import jax
        import jax.numpy as jnp
        _gk = jax.random.key(seed)
        x = -0.0005207 + 1.001 * jax.random.normal(jax.random.fold_in(_gk, 1), (64, 128, 256), jnp.float32)
        _a = jax.random.bernoulli(jax.random.fold_in(_gk, 2), 0.0625, (64, 128, 128))
        _a = jnp.logical_or(_a, jnp.swapaxes(_a, -1, -2))
        _a = jnp.logical_or(_a, jnp.eye(128, dtype=bool))
        adj = _a.astype(jnp.int32)
        return (x, adj)
    x, adj = _rec_inputs()

    def _L0_gnn_setup():
        import jax, jax.numpy as jnp
        import numpy as np
        B, S, D, H = (2, 1024, 256, 8)
        HD = D // H
        EPS = 1e-05

        def _ln(x, g, b):
            mu = jnp.mean(x, axis=-1, keepdims=True)
            var = jnp.mean((x - mu) ** 2, axis=-1, keepdims=True)
            return (x - mu) * jax.lax.rsqrt(var + EPS) * g + b
        key = jax.random.key(seed)
        ks = jax.random.split(key, 16)
        x = jax.random.normal(ks[0], (B, S, D), dtype=jnp.float32)
        adj = jax.random.randint(ks[1], (B, S, S), 0, 2, dtype=jnp.int32)
        adj = adj.at[:, jnp.arange(S), jnp.arange(S)].set(1)
        edge_attr = jax.random.normal(ks[2], (B, S, S), dtype=jnp.float32)
        sc = 1.0 / np.sqrt(D)
        p = lambda k, shp: jax.random.normal(k, shp, dtype=jnp.float32) * sc
        return {'x': x, 'adj_matrix': adj, 'edge_attr_matrix': edge_attr, 'ln1_g': jnp.ones((D,)), 'ln1_b': jnp.zeros((D,)), 'ln2_g': jnp.ones((D,)), 'ln2_b': jnp.zeros((D,)), 'wq': p(ks[3], (D, D)), 'bq': jnp.zeros((D,)), 'wk': p(ks[4], (D, D)), 'bk': jnp.zeros((D,)), 'wv': p(ks[5], (D, D)), 'bv': jnp.zeros((D,)), 'wo': p(ks[6], (D, D)), 'bo': jnp.zeros((D,)), 'w1': p(ks[7], (D, 4 * D)), 'b1': jnp.zeros((4 * D,)), 'w2': p(ks[8], (4 * D, D)), 'b2': jnp.zeros((D,))}
    _L0_gnn_all = _L0_gnn_setup()
    _L0_gnn_in = {k: v for k, v in _L0_gnn_all.items() if k in ('ln1_g', 'ln1_b', 'ln2_g', 'ln2_b', 'wq', 'bq', 'wk', 'bk', 'wv', 'bv', 'wo', 'bo', 'w1', 'b1', 'w2', 'b2')}
    del _L0_gnn_all
    return {'x': x, 'adj': adj, 'L0_gnn_ln1_g': _L0_gnn_in['ln1_g'], 'L0_gnn_ln1_b': _L0_gnn_in['ln1_b'], 'L0_gnn_ln2_g': _L0_gnn_in['ln2_g'], 'L0_gnn_ln2_b': _L0_gnn_in['ln2_b'], 'L0_gnn_wq': _L0_gnn_in['wq'], 'L0_gnn_bq': _L0_gnn_in['bq'], 'L0_gnn_wk': _L0_gnn_in['wk'], 'L0_gnn_bk': _L0_gnn_in['bk'], 'L0_gnn_wv': _L0_gnn_in['wv'], 'L0_gnn_bv': _L0_gnn_in['bv'], 'L0_gnn_wo': _L0_gnn_in['wo'], 'L0_gnn_bo': _L0_gnn_in['bo'], 'L0_gnn_w1': _L0_gnn_in['w1'], 'L0_gnn_b1': _L0_gnn_in['b1'], 'L0_gnn_w2': _L0_gnn_in['w2'], 'L0_gnn_b2': _L0_gnn_in['b2']}

def reference(x, adj, L0_gnn_ln1_g, L0_gnn_ln1_b, L0_gnn_ln2_g, L0_gnn_ln2_b, L0_gnn_wq, L0_gnn_bq, L0_gnn_wk, L0_gnn_bk, L0_gnn_wv, L0_gnn_bv, L0_gnn_wo, L0_gnn_bo, L0_gnn_w1, L0_gnn_b1, L0_gnn_w2, L0_gnn_b2):
    import jax
    import jax.numpy as jnp

    def _L0_gnn_ref(x, adj_matrix, edge_attr_matrix, ln1_g, ln1_b, ln2_g, ln2_b, wq, bq, wk, bk, wv, bv, wo, bo, w1, b1, w2, b2):
        import jax, jax.numpy as jnp
        import numpy as np
        B, S, D, H = (2, 1024, 256, 8)
        HD = D // H
        EPS = 1e-05

        def _ln(x, g, b):
            mu = jnp.mean(x, axis=-1, keepdims=True)
            var = jnp.mean((x - mu) ** 2, axis=-1, keepdims=True)
            return (x - mu) * jax.lax.rsqrt(var + EPS) * g + b
        b, s, d = x.shape
        residual = x
        nx = _ln(x, ln1_g, ln1_b)
        q = (nx @ wq + bq).reshape(b, s, H, HD).transpose(0, 2, 1, 3)
        k = (nx @ wk + bk).reshape(b, s, H, HD).transpose(0, 2, 1, 3)
        v = (nx @ wv + bv).reshape(b, s, H, HD).transpose(0, 2, 1, 3)
        adjf = adj_matrix.astype(jnp.float32)
        bias = jnp.where(adj_matrix > 0, 0.1 * edge_attr_matrix * adjf, -jnp.inf)[:, None]
        scores = jnp.einsum('bhqd,bhkd->bhqk', q, k) / np.sqrt(HD) + bias
        attn = jax.nn.softmax(scores, axis=-1)
        out = jnp.einsum('bhqk,bhkd->bhqd', attn, v)
        out = out.transpose(0, 2, 1, 3).reshape(b, s, d)
        x1 = residual + (out @ wo + bo)
        n2 = _ln(x1, ln2_g, ln2_b)
        mlp = jax.nn.gelu(n2 @ w1 + b1, approximate=False) @ w2 + b2
        return x1 + mlp
    x = _L0_gnn_ref(x, adj, adj, L0_gnn_ln1_g, L0_gnn_ln1_b, L0_gnn_ln2_g, L0_gnn_ln2_b, L0_gnn_wq, L0_gnn_bq, L0_gnn_wk, L0_gnn_bk, L0_gnn_wv, L0_gnn_bv, L0_gnn_wo, L0_gnn_bo, L0_gnn_w1, L0_gnn_b1, L0_gnn_w2, L0_gnn_b2)
    return x

_drawn_inputs = setup_inputs


def setup_inputs(seed=0):
    import zlib

    import numpy as np

    out = dict(_drawn_inputs(seed))
    spreads = {'L0_gnn_ln1_g': (1.0, 0.2),
     'L0_gnn_ln1_b': (0.0, 0.1),
     'L0_gnn_ln2_g': (1.0, 0.2),
     'L0_gnn_ln2_b': (0.0, 0.1),
     'L0_gnn_bq': (0.0, 0.267),
     'L0_gnn_bk': (0.0, 0.8),
     'L0_gnn_bv': (0.0, 0.1),
     'L0_gnn_bo': (0.0, 0.1),
     'L0_gnn_b1': (0.0, 0.1),
     'L0_gnn_b2': (0.0, 0.1)}
    factors = {}
    for name, (base, spread) in spreads.items():
        noise = np.random.default_rng([zlib.crc32(name.encode()), seed]).standard_normal(out[name].shape)
        drawn = base * np.exp(spread * noise) if base else spread * noise
        out[name] = jnp.asarray(drawn.astype(out[name].dtype))
    for name, factor in factors.items():
        out[name] = (out[name] * factor).astype(out[name].dtype)
    return out
```

```python
from contextlib import ExitStack

import concourse.bass as bass
from concourse import mybir

ALU = mybir.AluOpType
ACT = mybir.ActivationFunctionType
F32 = mybir.dt.float32
F32R = mybir.dt.float32r
I32 = mybir.dt.int32

P = 128
D = 256
DC = D // P
NH = 8
HD = D // NH
HC = P // HD
FF = 4 * D
FC = FF // P
GG = 4
T = GG * P
EPS = 1e-5
SCALE = float(HD) ** -0.5
MASKED = 1e30
UNIT = 8


def gnn_layer(nc, x, adj, ln1_g, ln1_b, ln2_g, ln2_b, wq, bq, wk, bk, wv, bv, wo, bo, w1, b1, w2, b2, out):
    NG = x.shape[0] // GG
    xs = x.rearrange("b s d -> (b s) d")
    adjs = adj.rearrange("b s t -> (b s) t")
    outs = out.rearrange("b s d -> (b s) d")
    ROWS = T // UNIT

    with ExitStack() as ctx:
        def sb(name, shape, dt=F32):
            return ctx.enter_context(nc.sbuf_tensor(name, shape, dt))

        def sem(name):
            return ctx.enter_context(nc.semaphore(name))

        raw = {n: sb(f"{n}_raw", [P, s[0], s[1]]) for n, s in
               dict(wq=(DC, D), wk=(DC, D), wv=(DC, D), wo=(DC, D), w1=(DC, FF), w2=(FC, D)).items()}
        hi = {n: sb(f"{n}_hi", list(t.shape), F32R) for n, t in raw.items()}
        lo = {n: sb(f"{n}_lo", list(t.shape), F32R) for n, t in raw.items()}
        ln_cols = sb("ln_cols", [P, 4, DC])
        bias_in = sb("bias_in", [P, 3 * DC + FC])
        bias_col = sb("bias_col", [P, 3 * DC + FC])
        bq_scaled = sb("bq_scaled", [P, DC])
        bo_row = sb("bo_row", [P, D])
        b2_row = sb("b2_row", [P, D])
        ident = sb("ident", [P, P])
        eps_t = sb("eps_t", [P, GG])
        mhalf = sb("mhalf", [P, GG])
        x_in = sb("x_in", [P, GG, D])
        adj_in = sb("adj_in", [P, GG, P], I32)
        adj_m = sb("adj_m", [P, GG, P])
        adj_e = sb("adj_e", [P, GG, P])
        edge_bias = sb("edge_bias", [P, GG, P])
        st1 = sb("st1", [P, GG, 6])
        mv1 = sb("mv1", [P, GG, 2])
        ve1 = sb("ve1", [P, GG])
        rs1 = sb("rs1", [P, GG])
        nx = sb("nx", [P, GG, D])
        nxT_hi = sb("nxT_hi", [P, DC, T], F32R)
        nxT_lo = sb("nxT_lo", [P, DC, T], F32R)
        qT = sb("qT", [P, DC, T])
        kT = sb("kT", [P, DC, T])
        v = sb("v", [P, GG, D])
        x_bo = sb("x_bo", [P, GG, D])
        sneg = sb("sneg", [P, NH, P])
        mneg = sb("mneg", [P, NH])
        prob = sb("prob", [P, NH, P])
        lsum = sb("lsum", [P, NH])
        rinv = sb("rinv", [P, NH])
        r_wide = sb("r_wide", [P, D])
        probT = sb("probT", [P, NH, P])
        rT = sb("rT", [P, DC, P])
        oT = sb("oT", [P, DC, P])
        oT_hi = sb("oT_hi", [P, DC, P], F32R)
        oT_lo = sb("oT_lo", [P, DC, P], F32R)
        x1 = sb("x1", [P, GG, D])
        st2 = sb("st2", [P, GG, 6])
        mv2 = sb("mv2", [P, GG, 2])
        ve2 = sb("ve2", [P, GG])
        rs2 = sb("rs2", [P, GG])
        n2 = sb("n2", [P, GG, D])
        x1_b2 = sb("x1_b2", [P, GG, D])
        n2T_hi = sb("n2T_hi", [P, DC, T], F32R)
        n2T_lo = sb("n2T_lo", [P, DC, T], F32R)
        h = sb("h", [P, 2, T])
        h_hi = sb("h_hi", [P, 2, T], F32R)
        h_lo = sb("h_lo", [P, 2, T], F32R)
        y = sb("y", [P, GG, D])

        att = ctx.enter_context(nc.psum_tensor("att", [P, 4, 512], F32))
        step = ctx.enter_context(nc.psum_tensor("step", [P, 2, 512], F32))
        mlp = ctx.enter_context(nc.psum_tensor("mlp", [P, 2, 512], F32))

        dma_small, dma_qkv, dma_rest = sem("dma_small"), sem("dma_qkv"), sem("dma_rest")
        d_alone, sp_alone = sem("d_alone"), sem("sp_alone")
        dma_x, dma_adj, dma_out = sem("dma_x"), sem("dma_adj"), sem("dma_out")
        p_ident, p_const = sem("p_ident"), sem("p_const")
        a_whi, d_wlo = sem("a_whi"), sem("d_wlo")
        s_bcol, d_bcol, s_bo, d_bo = sem("s_bcol"), sem("d_bcol"), sem("s_bo"), sem("d_bo")
        d_st1, d_mv1, p_ve1, p_rs1, d_nx = sem("d_st1"), sem("d_mv1"), sem("p_ve1"), sem("p_rs1"), sem("d_nx")
        s_nxT, a_nxT, d_nxT = sem("s_nxT"), sem("a_nxT"), sem("d_nxT")
        s_qk, a_qk, s_v, d_v = sem("s_qk"), sem("a_qk"), sem("s_v"), sem("d_v")
        d_adj, d_bias, p_xbo = sem("d_adj"), sem("d_bias"), sem("p_xbo")
        s_score, d_score, a_prob = sem("s_score"), sem("d_score"), sem("a_prob")
        s_probT, a_probT, d_probT = sem("s_probT"), sem("a_probT"), sem("d_probT")
        d_rinv, d_rwide, s_rT, a_rT = sem("d_rinv"), sem("d_rwide"), sem("s_rT"), sem("a_rT")
        s_oT, d_oT, a_oThi, d_oTlo = sem("s_oT"), sem("d_oT"), sem("a_oThi"), sem("d_oTlo")
        s_proj, d_x1, d_st2, d_mv2 = sem("s_proj"), sem("d_x1"), sem("d_st2"), sem("d_mv2")
        p_ve2, p_rs2, d_n2, p_x1b2 = sem("p_ve2"), sem("p_rs2"), sem("d_n2"), sem("p_x1b2")
        s_n2T, a_n2T, d_n2T = sem("s_n2T"), sem("a_n2T"), sem("d_n2T")
        s_up, a_h, d_hhi, d_hlo, s_down, d_y = (sem("s_up"), sem("a_h"), sem("d_hhi"), sem("d_hlo"),
                                                sem("s_down"), sem("d_y"))

        PER = UNIT // GG
        HALF = UNIT // DC

        def wait(eng, semaphore, value):
            if not isinstance(value, int) or value > 0:
                eng.wait_ge(semaphore, value)

        def split_product(psum, w, n_from, n_to, a_hi, a_lo, k, first, last, skip=False):
            for t, (l, r) in enumerate(((lo[w], a_hi), (hi[w], a_lo), (hi[w], a_hi))):
                mm = nc.tensor.matmul(psum, l[:, k, n_from:n_to], r, start=first and t == 0, stop=last and t == 2)
            return mm

        def split_product_rows(psum, a_hi, a_lo, w, k, first, last, skip=False):
            for t, (l, r) in enumerate(((a_hi, lo[w]), (a_lo, hi[w]), (a_hi, hi[w]))):
                mm = nc.tensor.matmul(psum, l, r[:, k, :], start=first and t == 0, stop=last and t == 2,
                                      skip_group_check=skip)
            return mm

        block = ctx.enter_context(nc.Block())

        def pipeline(eng, body):
            body(0, a=True, c=False)
            with eng.Fori(UNIT, UNIT * (NG - 3) + 1, UNIT) as base:
                body(base)
            body(UNIT * (NG - 2), load=False)
            body(UNIT * (NG - 1), a=False, load=False)
            body(UNIT * NG, a=False, b=False, load=False)

        @block.sync
        def _(sp):
            def load_x(g):
                sp.dma_start(x_in[:, :, :], xs[bass.ds(g * ROWS, T), :].rearrange("(j p) d -> p j d", p=P)).then_inc(dma_x, 16)

            def load_adj(g):
                sp.dma_start(adj_in[:, :, :], adjs[bass.ds(g * ROWS, T), :].rearrange("(j p) d -> p j d", p=P)).then_inc(dma_adj, 16)

            load_x(0)
            with nc.allow_non_contiguous_dma(reason="vectors onto partitions, once"):
                for n, vec in enumerate((ln1_g, ln1_b, ln2_g, ln2_b)):
                    sp.dma_start(ln_cols[:, n, :], vec.rearrange("(k p) -> p k", p=P)).then_inc(dma_small, 16)
                for n, vec in enumerate((bq, bk, bv, b1)):
                    k = vec.shape[0] // P
                    sp.dma_start(bias_in[:, DC * n:DC * n + k], vec.rearrange("(k p) -> p k", p=P)).then_inc(dma_small, 16)
            for dst, vec in ((bo_row, bo), (b2_row, b2)):
                sp.dma_start(dst[:, :], vec.rearrange("(a d) -> a d", a=1).to_broadcast([P, D])).then_inc(dma_small, 16)
            for n, w in (("wq", wq), ("wk", wk), ("wv", wv)):
                sp.dma_start(raw[n][:, :, :], w.rearrange("(k p) n -> p k n", p=P)).then_inc(dma_qkv, 16)
            load_adj(0)
            for n, w in (("wo", wo), ("w1", w1), ("w2", w2)):
                sp.dma_start(raw[n][:, :, :], w.rearrange("(k p) n -> p k n", p=P)).then_inc(dma_rest, 16)
            sp.wait_ge(d_nx, UNIT)
            sp.wait_ge(p_xbo, UNIT)
            load_x(UNIT)
            sp.wait_ge(d_bias, UNIT)
            load_adj(UNIT)

            def body(base, a=True, b=True, c=True, load=True):
                if c:
                    wait(sp, d_y, base)
                    sp.sem_inc(sp_alone, 1)
                    sp.dma_start(outs[bass.ds((base - UNIT) * ROWS, T), :].rearrange("(j p) d -> p j d", p=P),
                                 y[:, :, :]).then_inc(dma_out, 16)
                if load:
                    sp.wait_ge(d_nx, base + 2 * UNIT)
                    sp.wait_ge(p_xbo, base + 2 * UNIT)
                    sp.sem_inc(sp_alone, 1)
                    if c:
                        sp.wait_ge(dma_out, 2 * base)
                    sp.sem_inc(sp_alone, 1)
                    load_x(base + 2 * UNIT)
                    sp.wait_ge(d_bias, base + 2 * UNIT)
                    sp.sem_inc(sp_alone, 1)
                    load_adj(base + 2 * UNIT)

            pipeline(sp, body)
            sp.wait_ge(dma_out, 16 * NG)

        @block.gpsimd
        def _(pool):
            pool.memset(ident[:, :], 0.0).then_inc(p_const, 1)
            pool.memset(eps_t[:, :], EPS).then_inc(p_const, 1)
            pool.memset(mhalf[:, :], -0.5).then_inc(p_const, 1)
            pool.wait_ge(p_const, 3)
            pool.affine_select(out=ident[:, :], in_=ident[:, :], compare_op=ALU.not_equal, fill=1.0, base=0,
                               pattern=[[-1, P]], channel_multiplier=1).then_inc(p_ident, 1)

            def rstd(mv, ve, rs, js, d_mv, p_ve, p_rs, at, inc):
                j0, j1 = js
                pool.wait_ge(d_mv, at)
                pool.tensor_tensor(ve[:, j0:j1], mv[:, j0:j1, 1], eps_t[:, j0:j1], ALU.add).then_inc(p_ve, inc)
                pool.wait_ge(p_ve, at)
                pool.tensor_tensor(rs[:, j0:j1], ve[:, j0:j1], mhalf[:, j0:j1], ALU.pow).then_inc(p_rs, inc)

            def add_bo(ga, j):
                wait(pool, d_x1, ga - UNIT + PER * (j + 1))
                pool.tensor_tensor(x_bo[:, j, :], x_in[:, j, :], bo_row[:, :], ALU.add).then_inc(p_xbo, PER)

            rstd(mv1, ve1, rs1, (0, GG), d_mv1, p_ve1, p_rs1, UNIT, UNIT)
            pool.wait_ge(d_bo, 1)
            pool.wait_ge(dma_x, 16)
            for j in range(GG):
                add_bo(0, j)

            def body(base, a=True, b=True, c=True, load=True):
                for j in range(GG):
                    if b:
                        rstd(mv2, ve2, rs2, (j, j + 1), d_mv2, p_ve2, p_rs2, base + PER * (j + 1), PER)
                    if j == 1 and a:
                        rstd(mv1, ve1, rs1, (0, GG), d_mv1, p_ve1, p_rs1, base + 2 * UNIT, UNIT)
                if b:
                    for j in range(GG):
                        if j == 0:
                            wait(pool, d_y, base)
                        pool.tensor_tensor(x1_b2[:, j, :], x1[:, j, :], b2_row[:, :], ALU.add).then_inc(p_x1b2, PER)
                if a:
                    for j in range(GG):
                        add_bo(base + UNIT, j)

            pipeline(pool, body)

        @block.tensor
        def _(pe):
            pe.wait_ge(dma_small, 160)
            pe.wait_ge(dma_qkv, 48)
            pe.wait_ge(dma_rest, 48)
            col = 0
            for n, ln_b, chunks in (("wq", 1, DC), ("wk", 1, DC), ("wv", 1, DC), ("w1", 3, FC)):
                for m in range(chunks):
                    for k in range(DC):
                        mm = nc.tensor.matmul(att[:, 0, col:col + 1], raw[n][:, k, m * P:(m + 1) * P],
                                              ln_cols[:, ln_b, k:k + 1], start=(k == 0), stop=(k == DC - 1))
                    col += 1
            mm.then_inc(s_bcol, 1)
            pe.wait_ge(d_bcol, 1)
            for k in range(DC):
                mm = nc.tensor.matmul(att[:, 1, 0:D], bias_col[:, 2 * DC + k:2 * DC + k + 1].to_broadcast([P, P]),
                                      raw["wo"][:, k, :], start=(k == 0), stop=(k == DC - 1))
            mm.then_inc(s_bo, 1)
            pe.wait_ge(p_ident, 1)

            def nx_transpose(ga, k, free, at):
                if free is not None:
                    wait(pe, free, at)
                if k == 0:
                    pe.wait_ge(d_nx, ga + UNIT)
                for j in range(GG):
                    mm = nc.tensor.transpose(step[:, k, j * P:(j + 1) * P], nx[:, j, k * P:(k + 1) * P], ident[:, :])
                mm.then_inc(s_nxT, HALF)

            def project_qk(ga, m):
                if m == 0:
                    pe.wait_ge(d_nxT, ga + UNIT)
                if m >= 2:
                    pe.wait_ge(a_qk, ga + PER * (m - 1))
                w, c0 = ("wq", "wk")[m // DC], (m % DC) * P
                for k in range(DC):
                    mm = split_product(step[:, m % 2, :], w, c0, c0 + P, nxT_hi[:, k, :], nxT_lo[:, k, :], k,
                                       k == 0, k == DC - 1)
                mm.then_inc(s_qk, PER)

            def project_v(ga, j):
                if j < 2:
                    pe.wait_ge(a_qk, ga + PER * (j + 3))
                else:
                    pe.wait_ge(d_v, ga + PER * (j - 1))
                for k in range(DC):
                    mm = split_product_rows(step[:, j % 2, 0:D], nxT_hi[:, k, j * P:(j + 1) * P],
                                            nxT_lo[:, k, j * P:(j + 1) * P], "wv", k, k == 0, k == DC - 1)
                mm.then_inc(s_v, PER)

            def scores(g, j):
                if j == 0:
                    pe.wait_ge(a_qk, g + UNIT)
                wait(pe, d_x1, g + PER * j)
                for hh in range(NH):
                    r0 = (hh % HC) * HD
                    mm = nc.tensor.matmul(att[:, hh % 4, (hh // 4) * P:(hh // 4 + 1) * P],
                                          qT[r0:r0 + HD, hh // HC, j * P:(j + 1) * P],
                                          kT[r0:r0 + HD, hh // HC, j * P:(j + 1) * P], start=True, stop=True,
                                          tile_position=(r0, 0))
                mm.then_inc(s_score, PER)

            def prob_transpose(g, j):
                pe.wait_ge(d_score, g + PER * (j + 1))
                for half in range(2):
                    pe.wait_ge(a_prob, g + PER * j + half + 1)
                    for i in range(4):
                        mm = nc.tensor.transpose(att[:, half, i * P:(i + 1) * P], prob[:, 4 * half + i, :], ident[:, :])
                    mm.then_inc(s_probT, 1)
                pe.wait_ge(d_rwide, g + PER * (j + 1))
                for c in range(DC):
                    mm = nc.tensor.transpose(att[:, 2, c * P:(c + 1) * P], r_wide[:, c * P:(c + 1) * P], ident[:, :])
                mm.then_inc(s_rT, PER)

            def weigh_values(g, j):
                if j == 0:
                    pe.wait_ge(d_v, g + UNIT)
                pe.wait_ge(a_probT, g + PER * (j + 1))
                pe.wait_ge(d_probT, g + PER * (j + 1))
                for hh in range(NH):
                    p0 = (hh % HC) * HD
                    mm = nc.tensor.matmul(att[p0:p0 + HD, 3, (hh // HC) * P:(hh // HC + 1) * P],
                                          v[:, j, hh * HD:(hh + 1) * HD], probT[:, hh, :], start=True, stop=True,
                                          tile_position=(0, p0))
                mm.then_inc(s_oT, PER)

            def project_out(g, j):
                pe.wait_ge(a_rT, g + PER * (j + 1))
                pe.wait_ge(d_oTlo, g + PER * (j + 1))
                for k in range(DC):
                    mm = split_product_rows(att[:, 2, D:2 * D], oT_hi[:, k, :], oT_lo[:, k, :], "wo", k,
                                            k == 0, k == DC - 1)
                mm.then_inc(s_proj, PER)

            def n2_transpose(gc, k, free, at):
                pe.wait_ge(free, at)
                if k == 0:
                    pe.wait_ge(d_n2, gc + UNIT)
                for j in range(GG):
                    mm = nc.tensor.transpose(step[:, k, j * P:(j + 1) * P], n2[:, j, k * P:(k + 1) * P], ident[:, :])
                mm.then_inc(s_n2T, HALF)

            def mlp_up(gc, c):
                if c == 0:
                    pe.wait_ge(d_n2T, gc + UNIT)
                if c >= 2:
                    pe.wait_ge(a_h, gc + c - 1)
                for k in range(DC):
                    mm = split_product(step[:, c % 2, :], "w1", c * P, (c + 1) * P, n2T_hi[:, k, :], n2T_lo[:, k, :], k,
                                       k == 0, k == DC - 1)
                mm.then_inc(s_up, 1)

            def mlp_down(gc, c):
                pe.wait_ge(d_hlo, gc + c + 1)
                for j in range(GG):
                    mm = split_product_rows(mlp[:, j // 2, (j % 2) * D:(j % 2 + 1) * D],
                                            h_hi[:, c % 2, j * P:(j + 1) * P], h_lo[:, c % 2, j * P:(j + 1) * P],
                                            "w2", c, c == 0 and j % 2 == 0, c == FC - 1, skip=True)
                mm.then_inc(s_down, 1)

            pe.wait_ge(d_wlo, 3)
            for k in range(DC):
                nx_transpose(0, k, None, 0)
            for m in range(2 * DC):
                project_qk(0, m)
            for j in range(GG):
                project_v(0, j)
            pe.wait_ge(d_wlo, 6)
            pe.wait_ge(d_bo, 1)

            up, down = lambda c: ("up", c), lambda c: ("down", c)
            FILL = [
                [[("n2T", 0), ("n2T", 1)], [up(0)], [up(1)], [down(0), up(2)]],
                [[down(1), up(3)], [down(2), up(4)], [down(3)], [up(5)]],
                [[down(4), up(6)], [down(5), up(7)], [down(6)], [("nxT", 0), ("nxT", 1)]],
                [[down(7), ("qk", 0)], [("qk", 1)], [("qk", 2)], [("qk", 3)] + [("v", j) for j in range(GG)]],
            ]

            def body(base, a=True, b=True, c=True, load=True):
                def fill(kinds):
                    for kind, n in kinds:
                        if kind == "n2T" and c:
                            if b:
                                n2_transpose(base - UNIT, n, d_v, base + PER * (n + 3))
                            else:
                                n2_transpose(base - UNIT, n, a_h, base - 2 * UNIT + FC - 1 + n)
                        if kind == "up" and c:
                            mlp_up(base - UNIT, n)
                        if kind == "down" and c:
                            mlp_down(base - UNIT, n)
                        if kind == "nxT" and a:
                            if c:
                                nx_transpose(base + UNIT, n, a_h, base - UNIT + FC - 1 + n)
                            else:
                                nx_transpose(base + UNIT, n, d_v, base + PER * (n + 3))
                        if kind == "qk" and a:
                            project_qk(base + UNIT, n)
                        if kind == "v" and a:
                            project_v(base + UNIT, n)

                for j in range(GG):
                    for stage, filling in zip((scores, prob_transpose, weigh_values, project_out), FILL[j]):
                        if b:
                            stage(base, j)
                        fill(filling)

            pipeline(pe, body)

        @block.scalar
        def _(act):
            act.wait_ge(dma_small, 160)
            act.wait_ge(dma_qkv, 48)
            for n in ("wq", "wk", "wv"):
                for k in range(DC):
                    w = act.activation(hi[n][:, k, :], raw[n][:, k, :], ACT.Identity, scale=ln_cols[:, 0, k:k + 1])
                w.then_inc(a_whi, 1)
            act.wait_ge(dma_rest, 48)
            act.copy(hi["wo"][:, :, :], raw["wo"][:, :, :]).then_inc(a_whi, 1)
            for k in range(DC):
                w = act.activation(hi["w1"][:, k, :], raw["w1"][:, k, :], ACT.Identity, scale=ln_cols[:, 2, k:k + 1])
            w.then_inc(a_whi, 1)
            act.copy(hi["w2"][:, :, :], raw["w2"][:, :, :]).then_inc(a_whi, 1)

            def nxT_high(ga, k):
                act.wait_ge(s_nxT, ga + HALF * (k + 1))
                act.copy(nxT_hi[:, k, :], step[:, k, :]).then_inc(a_nxT, HALF)

            def qk_out(ga, m):
                act.wait_ge(s_qk, ga + PER * (m + 1))
                if m < DC:
                    i = act.activation(qT[:, m, :], step[:, m % 2, :], ACT.Identity, bias=bq_scaled[:, m:m + 1],
                                       scale=SCALE)
                else:
                    i = act.activation(kT[:, m - DC, :], step[:, m % 2, :], ACT.Identity, bias=bias_col[:, m:m + 1])
                i.then_inc(a_qk, PER)

            def n2T_high(gc, k):
                act.wait_ge(s_n2T, gc + HALF * (k + 1))
                act.copy(n2T_hi[:, k, :], step[:, k, :]).then_inc(a_n2T, HALF)

            def gelu(gc, c):
                act.wait_ge(s_up, gc + c + 1)
                if c >= 2:
                    act.wait_ge(d_hlo, gc + c - 1)
                act.activation(h[:, c % 2, :], step[:, c % 2, :], ACT.Gelu,
                               bias=bias_col[:, 3 * DC + c:3 * DC + c + 1]).then_inc(a_h, 1)

            def softmax(g, j):
                for half in range(2):
                    act.wait_ge(d_score, g + PER * j + half + 1)
                    for hh in range(4 * half, 4 * half + 4):
                        i = act.activation(prob[:, hh, :], sneg[:, hh, :], ACT.Exp, bias=mneg[:, hh:hh + 1],
                                           scale=-1.0, accum_out=lsum[:, hh:hh + 1])
                    i.then_inc(a_prob, 1)

            def probT_out(g, j):
                act.wait_ge(s_probT, g + PER * j + 1)
                act.copy(probT[:, 0:4, :], att[:, 0, :].rearrange("p (h q) -> p h q", h=4)).then_inc(a_probT, PER)
                act.wait_ge(s_rT, g + PER * (j + 1))
                act.copy(rT[:, :, :], att[:, 2, 0:D].rearrange("p (c q) -> p c q", c=DC)).then_inc(a_rT, PER)

            def oT_high(g, j):
                act.wait_ge(d_oT, g + PER * (j + 1))
                act.copy(oT_hi[:, :, :], oT[:, :, :]).then_inc(a_oThi, PER)

            act.wait_ge(d_bcol, 2)
            for k in range(DC):
                nxT_high(0, k)
            for m in range(2 * DC):
                qk_out(0, m)

            def body(base, a=True, b=True, c=True, load=True):
                for j in range(GG):
                    gc, ga = base - UNIT, base + UNIT
                    if c and j == 0:
                        for k in range(DC):
                            n2T_high(gc, k)
                    if b:
                        softmax(base, j)
                    if a and j == 3:
                        qk_out(ga, 0)
                    if b:
                        probT_out(base, j)
                    if c and j < 3:
                        gelu(gc, (0, 3, 6)[j])
                    if c and j in (1, 2):
                        gelu(gc, (0, 4, 7)[j])
                    if a and j == 3:
                        qk_out(ga, 1)
                    if b:
                        oT_high(base, j)
                    if c and j < 2:
                        gelu(gc, (1, 5)[j])
                    if c and j == 0:
                        gelu(gc, 2)
                    if a and j == 2:
                        for k in range(DC):
                            nxT_high(ga, k)
                    if a and j == 3:
                        qk_out(ga, 2)
                        qk_out(ga, 3)

            pipeline(act, body)

        @block.vector
        def _(dve):
            def low(out_, full, high):
                return dve.tensor_tensor(out_, full, high.bitcast(F32), ALU.subtract)

            def ln_stats(src, st, mv, js, d_st, d_mv, at, inc):
                for j in js:
                    i = dve.bn_stats(st[:, j, :], src[:, j, :])
                i.then_inc(d_st, inc)
                dve.wait_ge(d_st, at)
                dve.sem_inc(d_alone, 1)
                for j in js:
                    i = dve.bn_aggr(mv[:, j, :], st[:, j, :])
                i.then_inc(d_mv, inc)

            def ln1_stats(ga):
                dve.wait_ge(dma_x, 2 * ga + 16)
                ln_stats(x_in, st1, mv1, range(GG), d_st1, d_mv1, ga + UNIT, UNIT)

            def ln1_apply(ga):
                dve.wait_ge(p_rs1, ga + UNIT)
                for j in range(GG):
                    i = dve.tensor_scalar(nx[:, j, :], x_in[:, j, :], mv1[:, j, 0:1], rs1[:, j:j + 1],
                                          ALU.subtract, ALU.mult)
                i.then_inc(d_nx, UNIT)

            def nxT_low(ga, k):
                dve.wait_ge(a_nxT, ga + HALF * (k + 1))
                low(nxT_lo[:, k, :], step[:, k, :], nxT_hi[:, k, :]).then_inc(d_nxT, HALF)

            def v_out(ga, j):
                dve.wait_ge(s_v, ga + PER * (j + 1))
                dve.tensor_copy(v[:, j, :], step[:, j % 2, 0:D]).then_inc(d_v, PER)

            def edges(ga):
                dve.wait_ge(dma_adj, 2 * ga + 16)
                dve.tensor_scalar(adj_m[:, :, :], adj_in[:, :, :], 0.0, 1.0, ALU.is_gt, ALU.subtract).then_inc(d_adj, HALF)
                dve.scalar_tensor_tensor(out=adj_e[:, :, :], in0=adj_in[:, :, :], scalar=0.1, in1=adj_in[:, :, :],
                                         op0=ALU.mult, op1=ALU.mult).then_inc(d_adj, HALF)
                dve.wait_ge(d_adj, ga + UNIT)
                dve.scalar_tensor_tensor(out=edge_bias[:, :, :], in0=adj_m[:, :, :], scalar=MASKED, in1=adj_e[:, :, :],
                                         op0=ALU.mult, op1=ALU.add).then_inc(d_bias, UNIT)

            def score_max(g, j):
                if j == 0:
                    dve.wait_ge(d_bias, g + UNIT)
                dve.wait_ge(s_score, g + PER * (j + 1))
                dve.sem_inc(d_alone, 1)
                for hh in range(NH):
                    i = dve.tensor_tensor_reduce(out=sneg[:, hh, :], in0=att[:, hh % 4, (hh // 4) * P:(hh // 4 + 1) * P],
                                                 in1=edge_bias[:, j, :], scale=-1.0, scalar=3e38, op0=ALU.add,
                                                 op1=ALU.min, accum_out=mneg[:, hh:hh + 1])
                    if hh % 4 == 3:
                        i.then_inc(d_score, 1)

            def sums_inverse(g, j):
                dve.wait_ge(a_prob, g + PER * (j + 1))
                dve.reciprocal(rinv[:, :], lsum[:, :]).then_inc(d_rinv, PER)
                dve.wait_ge(d_rinv, g + PER * (j + 1))
                dve.tensor_copy(r_wide[:, :].rearrange("p (h d) -> p h d", h=NH),
                                rinv[:, :].unsqueeze(2).to_broadcast([P, NH, HD])).then_inc(d_rwide, PER)

            def probT_out(g, j):
                dve.wait_ge(s_probT, g + PER * (j + 1))
                dve.tensor_copy(probT[:, 4:8, :], att[:, 1, :].rearrange("p (h q) -> p h q", h=4)).then_inc(d_probT, PER)

            def normalise(g, j):
                dve.wait_ge(s_oT, g + PER * (j + 1))
                dve.wait_ge(a_rT, g + PER * (j + 1))
                dve.tensor_tensor(oT[:, :, :], att[:, 3, 0:D].rearrange("p (c q) -> p c q", c=DC), rT[:, :, :],
                                  ALU.mult).then_inc(d_oT, PER)
                dve.wait_ge(a_oThi, g + PER * (j + 1))
                low(oT_lo[:, :, :], oT[:, :, :], oT_hi[:, :, :]).then_inc(d_oTlo, PER)

            def residual(g, j):
                dve.wait_ge(p_xbo, g + PER * (j + 1))
                wait(dve, p_x1b2, g - UNIT + PER * (j + 1))
                dve.wait_ge(s_proj, g + PER * (j + 1))
                dve.tensor_tensor(x1[:, j, :], att[:, 2, D:2 * D], x_bo[:, j, :], ALU.add).then_inc(d_x1, PER)
                dve.wait_ge(d_x1, g + PER * (j + 1))
                ln_stats(x1, st2, mv2, (j,), d_st2, d_mv2, g + PER * (j + 1), PER)

            def ln2_apply(g, j):
                dve.wait_ge(p_rs2, g + PER * (j + 1))
                dve.tensor_scalar(n2[:, j, :], x1[:, j, :], mv2[:, j, 0:1], rs2[:, j:j + 1], ALU.subtract,
                                  ALU.mult).then_inc(d_n2, PER)

            def n2T_low(gc, k):
                dve.wait_ge(a_n2T, gc + HALF * (k + 1))
                low(n2T_lo[:, k, :], step[:, k, :], n2T_hi[:, k, :]).then_inc(d_n2T, HALF)

            def h_split(gc, c):
                dve.wait_ge(a_h, gc + c + 1)
                if c >= 2:
                    dve.wait_ge(s_down, gc + c - 1)
                dve.tensor_copy(h_hi[:, c % 2, :], h[:, c % 2, :]).then_inc(d_hhi, 1)
                dve.wait_ge(d_hhi, gc + c + 1)
                low(h_lo[:, c % 2, :], h[:, c % 2, :], h_hi[:, c % 2, :]).then_inc(d_hlo, 1)

            def y_out(gc, load):
                dve.wait_ge(s_down, gc + UNIT)
                dve.wait_ge(p_x1b2, gc + UNIT)
                if not load:
                    wait(dve, dma_out, 2 * gc)
                for half in range(2):
                    dve.tensor_tensor(y[:, 2 * half:2 * half + 2, :], mlp[:, half, :].rearrange("p (j d) -> p j d", j=2),
                                      x1_b2[:, 2 * half:2 * half + 2, :], ALU.add).then_inc(d_y, HALF)

            ln1_stats(0)
            dve.wait_ge(dma_small, 160)
            for m, n in enumerate(("wq", "wk", "wv")):
                dve.wait_ge(a_whi, m + 1)
                for k in range(DC):
                    i = dve.scalar_tensor_tensor(out=lo[n][:, k, :], in0=raw[n][:, k, :], scalar=ln_cols[:, 0, k:k + 1],
                                                 in1=hi[n][:, k, :].bitcast(F32), op0=ALU.mult, op1=ALU.subtract)
                i.then_inc(d_wlo, 1)
            ln1_apply(0)
            dve.wait_ge(s_bcol, 1)
            dve.tensor_tensor(bias_col[:, :], att[:, 0, 0:3 * DC + FC], bias_in[:, :], ALU.add).then_inc(d_bcol, 1)
            dve.wait_ge(d_bcol, 1)
            dve.tensor_scalar(bq_scaled[:, :], bias_col[:, 0:DC], SCALE, None, ALU.mult).then_inc(d_bcol, 1)
            dve.wait_ge(s_bo, 1)
            dve.tensor_tensor(bo_row[:, :], att[:, 1, 0:D], bo_row[:, :], ALU.add).then_inc(d_bo, 1)
            for k in range(DC):
                nxT_low(0, k)
            edges(0)
            dve.wait_ge(a_whi, 4)
            low(lo["wo"][:, :, :], raw["wo"][:, :, :], hi["wo"][:, :, :]).then_inc(d_wlo, 1)
            for j in range(GG):
                v_out(0, j)
            dve.wait_ge(a_whi, 6)
            for k in range(DC):
                i = dve.scalar_tensor_tensor(out=lo["w1"][:, k, :], in0=raw["w1"][:, k, :], scalar=ln_cols[:, 2, k:k + 1],
                                             in1=hi["w1"][:, k, :].bitcast(F32), op0=ALU.mult, op1=ALU.subtract)
            i.then_inc(d_wlo, 1)
            low(lo["w2"][:, :, :], raw["w2"][:, :, :], hi["w2"][:, :, :]).then_inc(d_wlo, 1)

            def body(base, a=True, b=True, c=True, load=True):
                gc, ga = base - UNIT, base + UNIT
                for j in range(GG):
                    if b:
                        score_max(base, j)
                    if c and j == 0:
                        for k in range(DC):
                            n2T_low(gc, k)
                    if a and j == 1:
                        ln1_stats(ga)
                    if c and j == 2:
                        h_split(gc, 5)
                    if c and j == 3:
                        y_out(gc, load)
                    if b:
                        sums_inverse(base, j)
                    if a and j == 2:
                        ln1_apply(ga)
                    if b:
                        probT_out(base, j)
                    if c and j in (1, 2):
                        h_split(gc, (0, 3, 6)[j])
                    if b:
                        normalise(base, j)
                    if c and j < 3:
                        h_split(gc, (0, 4, 7)[j])
                    if b:
                        residual(base, j)
                    if c and j == 0:
                        h_split(gc, 1)
                    if a and j == 3:
                        v_out(ga, 0)
                        v_out(ga, 1)
                    if b:
                        ln2_apply(base, j)
                    if c and j == 0:
                        h_split(gc, 2)
                    if a and j == 2:
                        for k in range(DC):
                            nxT_low(ga, k)
                    if a and j == 3:
                        v_out(ga, 2)
                        v_out(ga, 3)
                        edges(ga)

            pipeline(dve, body)


_INS = ['x', 'adj'] + ['L0_gnn_' + n for n in ('ln1_g', 'ln1_b', 'ln2_g', 'ln2_b', 'wq', 'bq', 'wk', 'bk', 'wv', 'bv',
                                              'wo', 'bo', 'w1', 'b1', 'w2', 'b2')]
_OUTS = [((64, 128, 256), 'float32')]


def kernel(**inputs):
    import numpy as _np
    import concourse.bacc as _bacc
    from concourse import mybir as _mybir
    from concourse.bass_utils import run_bass_kernel_spmd as _run

    nc = _bacc.Bacc("TRN2", target_bir_lowering=False, num_devices=1)
    arrays, args = {}, []
    for name in _INS:
        a = _np.ascontiguousarray(inputs[name])
        arrays[f"in_{name}_dram"] = a
        args.append(nc.dram_tensor(f"in_{name}_dram", a.shape, _mybir.dt.from_np(a.dtype), kind="ExternalInput").ap())
    for i, (shape, dtype) in enumerate(_OUTS):
        dt = _mybir.dt.from_np(_np.dtype(dtype))
        args.append(nc.dram_tensor(f"out_{i}_dram", shape, dt, kind="ExternalOutput").ap())
    gnn_layer(nc, *args)
    r = _run(nc, [arrays], core_ids=[0])
    got = tuple(r.results[0][f"out_{i}_dram"] for i in range(len(_OUTS)))
    return got[0]
```

```python
from contextlib import ExitStack

import concourse.bass as bass
from concourse import mybir

ALU = mybir.AluOpType
ACT = mybir.ActivationFunctionType
F32 = mybir.dt.float32
F32R = mybir.dt.float32r
I32 = mybir.dt.int32

P = 128
D = 256
DC = D // P
NH = 8
HD = D // NH
HC = P // HD
FF = 4 * D
FC = FF // P
GG = 4
T = GG * P
HB = 4
EPS = 1e-5
SCALE = float(HD) ** -0.5
MASKED = 1e30
UNIT = 8


def gnn_layer(nc, x, adj, ln1_g, ln1_b, ln2_g, ln2_b, wq, bq, wk, bk, wv, bv, wo, bo, w1, b1, w2, b2, out):
    NG = x.shape[0] // GG
    xs = x.rearrange("b s d -> (b s) d")
    adjs = adj.rearrange("b s t -> (b s) t")
    outs = out.rearrange("b s d -> (b s) d")
    ROWS = T // UNIT

    with ExitStack() as ctx:
        def sb(name, shape, dt=F32):
            return ctx.enter_context(nc.sbuf_tensor(name, shape, dt))

        def sem(name):
            return ctx.enter_context(nc.semaphore(name))

        raw = {n: sb(f"{n}_raw", [P, s[0], s[1]]) for n, s in
               dict(wq=(DC, D), wk=(DC, D), wv=(DC, D), wo=(DC, D), w1=(DC, FF), w2=(FC, D)).items()}
        hi = {n: sb(f"{n}_hi", list(t.shape), F32R) for n, t in raw.items()}
        lo = {n: sb(f"{n}_lo", list(t.shape), F32R) for n, t in raw.items()}
        ln_cols = sb("ln_cols", [P, 4, DC])
        bias_in = sb("bias_in", [P, 3 * DC + FC])
        bias_col = sb("bias_col", [P, 3 * DC + FC])
        bq_scaled = sb("bq_scaled", [P, DC])
        bo_row = sb("bo_row", [P, D])
        b2_row = sb("b2_row", [P, D])
        ident = sb("ident", [P, P])
        eps_t = sb("eps_t", [P, GG])
        mhalf = sb("mhalf", [P, GG])
        x_in = sb("x_in", [P, GG, D])
        adj_in = sb("adj_in", [P, GG, P], I32)
        adj_m = sb("adj_m", [P, GG, P])
        adj_e = sb("adj_e", [P, GG, P])
        edge_bias = sb("edge_bias", [P, GG, P])
        st1 = sb("st1", [P, GG, 6])
        mv1 = sb("mv1", [P, GG, 2])
        ve1 = sb("ve1", [P, GG])
        rs1 = sb("rs1", [P, GG])
        nx = sb("nx", [P, GG, D])
        nxT_hi = sb("nxT_hi", [P, DC, T], F32R)
        nxT_lo = sb("nxT_lo", [P, DC, T], F32R)
        qT = sb("qT", [P, DC, T])
        kT = sb("kT", [P, DC, T])
        v = sb("v", [P, GG, D])
        x_bo = sb("x_bo", [P, GG, D])
        sneg = sb("sneg", [P, NH, P])
        mneg = sb("mneg", [P, NH])
        prob = sb("prob", [P, 2, NH, P])
        lsum = sb("lsum", [P, NH])
        rinv = sb("rinv", [P, NH])
        probT = sb("probT", [P, NH, P])
        oT_hi = sb("oT_hi", [P, DC, P], F32R)
        oT_lo = sb("oT_lo", [P, DC, P], F32R)
        x1 = sb("x1", [P, GG, D])
        st2 = sb("st2", [P, GG, 6])
        mv2 = sb("mv2", [P, GG, 2])
        ve2 = sb("ve2", [P, GG])
        rs2 = sb("rs2", [P, GG])
        n2 = sb("n2", [P, GG, D])
        x1_b2 = sb("x1_b2", [P, 2 * GG * D])
        n2T_hi = sb("n2T_hi", [P, DC, T], F32R)
        n2T_lo = sb("n2T_lo", [P, DC, T], F32R)
        h = sb("h", [P, 2, T])
        h_hi = sb("h_hi", [P, HB, T], F32R)
        h_lo = sb("h_lo", [P, HB, T], F32R)
        y = sb("y", [P, GG, D])

        att = ctx.enter_context(nc.psum_tensor("att", [P, 4, 512], F32))
        step = ctx.enter_context(nc.psum_tensor("step", [P, 2, 512], F32))
        mlp = ctx.enter_context(nc.psum_tensor("mlp", [P, 2, 512], F32))

        dma_small, dma_qkv, dma_rest = sem("dma_small"), sem("dma_qkv"), sem("dma_rest")
        d_alone, sp_alone, p_alone = sem("d_alone"), sem("sp_alone"), sem("p_alone")
        dma_x, dma_adj, dma_out = sem("dma_x"), sem("dma_adj"), sem("dma_out")
        p_ident, p_const = sem("p_ident"), sem("p_const")
        a_whi, d_wlo = sem("a_whi"), sem("d_wlo")
        s_bcol, d_bcol, s_bo, d_bo = sem("s_bcol"), sem("d_bcol"), sem("s_bo"), sem("d_bo")
        d_st1, d_mv1, p_ve1, p_rs1, d_nx = sem("d_st1"), sem("d_mv1"), sem("p_ve1"), sem("p_rs1"), sem("d_nx")
        s_nxT, a_nxT, d_nxT = sem("s_nxT"), sem("a_nxT"), sem("d_nxT")
        s_qk, a_qk, s_v, d_v = sem("s_qk"), sem("a_qk"), sem("s_v"), sem("d_v")
        d_adj, d_bias, p_xbo = sem("d_adj"), sem("d_bias"), sem("p_xbo")
        s_score, d_score, a_prob = sem("s_score"), sem("d_score"), sem("a_prob")
        s_probT, d_probT = sem("s_probT"), sem("d_probT")
        d_rinv, p_prob = sem("d_rinv"), sem("p_prob")
        s_oT, a_oThi, d_oTlo = sem("s_oT"), sem("a_oThi"), sem("d_oTlo")
        s_proj, d_x1, d_st2, d_mv2 = sem("s_proj"), sem("d_x1"), sem("d_st2"), sem("d_mv2")
        p_ve2, p_rs2, d_n2, p_x1b2 = sem("p_ve2"), sem("p_rs2"), sem("d_n2"), sem("p_x1b2")
        s_n2T, a_n2T, d_n2T = sem("s_n2T"), sem("a_n2T"), sem("d_n2T")
        s_up, a_h, d_hhi, d_hlo, s_down, d_y = (sem("s_up"), sem("a_h"), sem("d_hhi"), sem("d_hlo"),
                                                sem("s_down"), sem("d_y"))

        PER = UNIT // GG
        HALF = UNIT // DC

        def wait(eng, semaphore, value):
            if not isinstance(value, int) or value > 0:
                eng.wait_ge(semaphore, value)

        def split_product(psum, w, n_from, n_to, a_hi, a_lo, k, first, last, skip=False):
            for t, (l, r) in enumerate(((lo[w], a_hi), (hi[w], a_lo), (hi[w], a_hi))):
                mm = nc.tensor.matmul(psum, l[:, k, n_from:n_to], r, start=first and t == 0, stop=last and t == 2)
            return mm

        def split_product_rows(psum, a_hi, a_lo, w, k, first, last, skip=False):
            for t, (l, r) in enumerate(((a_hi, lo[w]), (a_lo, hi[w]), (a_hi, hi[w]))):
                mm = nc.tensor.matmul(psum, l, r[:, k, :], start=first and t == 0, stop=last and t == 2,
                                      skip_group_check=skip)
            return mm

        block = ctx.enter_context(nc.Block())

        FIRST, LAST = 3, NG - 2

        def pipeline(eng, body):
            for i in range(FIRST):
                body(UNIT * i, lambda k: 0 <= i + k < NG)
            with eng.Fori(UNIT * FIRST, UNIT * LAST + 1, UNIT) as base:
                body(base, lambda k: True)
            for i in range(LAST + 1, NG + 2):
                body(UNIT * i, lambda k: 0 <= i + k < NG)

        @block.sync
        def _(sp):
            def load_x(g):
                sp.dma_start(x_in[:, :, :], xs[bass.ds(g * ROWS, T), :].rearrange("(j p) d -> p j d", p=P)).then_inc(dma_x, 16)

            def load_adj(g):
                sp.dma_start(adj_in[:, :, :], adjs[bass.ds(g * ROWS, T), :].rearrange("(j p) d -> p j d", p=P)).then_inc(dma_adj, 16)

            load_x(0)
            with nc.allow_non_contiguous_dma(reason="vectors onto partitions, once"):
                for n, vec in enumerate((ln1_g, ln1_b, ln2_g, ln2_b)):
                    sp.dma_start(ln_cols[:, n, :], vec.rearrange("(k p) -> p k", p=P)).then_inc(dma_small, 16)
                for n, vec in enumerate((bq, bk, bv, b1)):
                    k = vec.shape[0] // P
                    sp.dma_start(bias_in[:, DC * n:DC * n + k], vec.rearrange("(k p) -> p k", p=P)).then_inc(dma_small, 16)
            for dst, vec in ((bo_row, bo), (b2_row, b2)):
                sp.dma_start(dst[:, :], vec.rearrange("(a d) -> a d", a=1).to_broadcast([P, D])).then_inc(dma_small, 16)
            for n, w in (("wq", wq), ("wk", wk), ("wv", wv)):
                sp.dma_start(raw[n][:, :, :], w.rearrange("(k p) n -> p k n", p=P)).then_inc(dma_qkv, 16)
            load_adj(0)
            for n, w in (("wo", wo), ("w1", w1), ("w2", w2)):
                sp.dma_start(raw[n][:, :, :], w.rearrange("(k p) n -> p k n", p=P)).then_inc(dma_rest, 16)

            def body(base, has):
                if has(1):
                    sp.wait_ge(d_nx, base + UNIT)
                    sp.wait_ge(p_xbo, base + UNIT)
                    sp.sem_inc(sp_alone, 1)
                    load_x(base + UNIT)
                    sp.wait_ge(d_bias, base + UNIT)
                    sp.sem_inc(sp_alone, 1)
                    load_adj(base + UNIT)
                if has(-2):
                    sp.wait_ge(d_y, base - UNIT)
                    sp.sem_inc(sp_alone, 1)
                    sp.dma_start(outs[bass.ds((base - 2 * UNIT) * ROWS, T), :].rearrange("(j p) d -> p j d", p=P),
                                 y[:, :, :]).then_inc(dma_out, 16)

            pipeline(sp, body)
            sp.wait_ge(dma_out, 16 * NG)

        @block.gpsimd
        def _(pool):
            pool.memset(ident[:, :], 0.0).then_inc(p_const, 1)
            pool.memset(eps_t[:, :], EPS).then_inc(p_const, 1)
            pool.memset(mhalf[:, :], -0.5).then_inc(p_const, 1)
            pool.wait_ge(p_const, 3)
            pool.affine_select(out=ident[:, :], in_=ident[:, :], compare_op=ALU.not_equal, fill=1.0, base=0,
                               pattern=[[-1, P]], channel_multiplier=1).then_inc(p_ident, 1)

            def rstd(mv, ve, rs, js, d_mv, p_ve, p_rs, at, inc):
                j0, j1 = js
                pool.wait_ge(d_mv, at)
                pool.tensor_tensor(ve[:, j0:j1], mv[:, j0:j1, 1], eps_t[:, j0:j1], ALU.add).then_inc(p_ve, inc)
                pool.wait_ge(p_ve, at)
                pool.tensor_tensor(rs[:, j0:j1], ve[:, j0:j1], mhalf[:, j0:j1], ALU.pow).then_inc(p_rs, inc)

            def add_bo(ga, j):
                wait(pool, d_x1, ga - UNIT + PER * (j + 1))
                pool.wait_ge(dma_x, 2 * ga + 16)
                pool.tensor_tensor(x_bo[:, j, :], x_in[:, j, :], bo_row[:, :], ALU.add).then_inc(p_xbo, PER)

            def add_b2(g, j):
                pool.wait_ge(d_x1, g + PER * (j + 1))
                wait(pool, d_y, g - UNIT)
                pool.sem_inc(p_alone, 1)
                pool.tensor_tensor(x1_b2[:, bass.ds(((g // UNIT) % 2) * (GG * D) + j * D, D)], x1[:, j, :],
                                   b2_row[:, :], ALU.add).then_inc(p_x1b2, PER)

            def scale_prob(g, j):
                pool.wait_ge(d_rinv, g + PER * (j + 1))
                for half in range(2):
                    heads = slice(4 * half, 4 * half + 4)
                    pool.tensor_tensor(prob[:, j % 2, heads, :], prob[:, j % 2, heads, :],
                                       rinv[:, heads].unsqueeze(2).to_broadcast([P, 4, P]), ALU.mult).then_inc(p_prob, 1)

            def rstd2(g, j):
                rstd(mv2, ve2, rs2, (j, j + 1), d_mv2, p_ve2, p_rs2, g + PER * (j + 1), PER)

            rstd(mv1, ve1, rs1, (0, GG), d_mv1, p_ve1, p_rs1, UNIT, UNIT)
            pool.wait_ge(d_bo, 1)
            for j in range(GG):
                add_bo(0, j)

            def body(base, has):
                if has(0):
                    scale_prob(base, 0)
                if has(-1):
                    rstd2(base - UNIT, 3)
                    if has(0):
                        add_bo(base, 3)
                    add_b2(base - UNIT, 3)
                if has(0):
                    scale_prob(base, 1)
                    rstd2(base, 0)
                if has(1):
                    rstd(mv1, ve1, rs1, (0, GG), d_mv1, p_ve1, p_rs1, base + 2 * UNIT, UNIT)
                    add_bo(base + UNIT, 0)
                if has(0):
                    scale_prob(base, 2)
                    rstd2(base, 1)
                    add_b2(base, 0)
                    add_b2(base, 1)
                if has(1):
                    add_bo(base + UNIT, 1)
                if has(0):
                    scale_prob(base, 3)
                    rstd2(base, 2)
                    add_b2(base, 2)
                if has(1):
                    add_bo(base + UNIT, 2)

            pipeline(pool, body)

        @block.tensor
        def _(pe):
            pe.wait_ge(dma_small, 160)
            pe.wait_ge(dma_qkv, 48)
            pe.wait_ge(dma_rest, 48)
            col = 0
            for n, ln_b, chunks in (("wq", 1, DC), ("wk", 1, DC), ("wv", 1, DC), ("w1", 3, FC)):
                for m in range(chunks):
                    for k in range(DC):
                        mm = nc.tensor.matmul(att[:, 0, col:col + 1], raw[n][:, k, m * P:(m + 1) * P],
                                              ln_cols[:, ln_b, k:k + 1], start=(k == 0), stop=(k == DC - 1))
                    col += 1
            mm.then_inc(s_bcol, 1)
            pe.wait_ge(d_bcol, 1)
            for k in range(DC):
                mm = nc.tensor.matmul(att[:, 1, 0:D], bias_col[:, 2 * DC + k:2 * DC + k + 1].to_broadcast([P, P]),
                                      raw["wo"][:, k, :], start=(k == 0), stop=(k == DC - 1))
            mm.then_inc(s_bo, 1)
            pe.wait_ge(p_ident, 1)

            def nx_transpose(ga, k, freed=None):
                if freed is not None:
                    pe.wait_ge(a_h, freed)
                if k == 0:
                    pe.wait_ge(d_nx, ga + UNIT)
                for j in range(GG):
                    mm = nc.tensor.transpose(step[:, k, j * P:(j + 1) * P], nx[:, j, k * P:(k + 1) * P], ident[:, :])
                mm.then_inc(s_nxT, HALF)

            def project_qk(ga, m):
                if m == 0:
                    pe.wait_ge(d_nxT, ga + UNIT)
                if m >= 2:
                    pe.wait_ge(a_qk, ga + PER * (m - 1))
                w, c0 = ("wq", "wk")[m % 2], (m // 2) * P
                for k in range(DC):
                    mm = split_product(step[:, m % 2, :], w, c0, c0 + P, nxT_hi[:, k, :], nxT_lo[:, k, :], k,
                                       k == 0, k == DC - 1)
                mm.then_inc(s_qk, PER)

            def project_v(g, j):
                to = att[:, 3 if j == 3 else 2, D:2 * D]
                for k in range(DC):
                    mm = split_product_rows(to, nxT_hi[:, k, j * P:(j + 1) * P],
                                            nxT_lo[:, k, j * P:(j + 1) * P], "wv", k, k == 0, k == DC - 1)
                mm.then_inc(s_v, PER)

            def scores(g, j):
                wait(pe, d_oTlo, g + PER * (j - 1))
                for hh in (0, 1, 3, 4, 5, 7, 2, 6):
                    if j == 0 and hh in (0, 4):
                        pe.wait_ge(a_qk, g + 2 * PER * (hh // HC + 1))
                    if hh == 2:
                        wait(pe, d_x1, g + PER * (j - 1))
                    r0 = (hh % HC) * HD
                    mm = nc.tensor.matmul(att[:, hh % 4, (hh // 4) * P:(hh // 4 + 1) * P],
                                          qT[r0:r0 + HD, hh // HC, j * P:(j + 1) * P],
                                          kT[r0:r0 + HD, hh // HC, j * P:(j + 1) * P], start=True, stop=True,
                                          tile_position=(r0, 0))
                mm.then_inc(s_score, PER)

            def prob_transpose(g, j, others):
                if others is not None:
                    pe.wait_ge(d_score, others)
                else:
                    pe.wait_ge(d_x1, g + PER * j)
                for half in range(2):
                    pe.wait_ge(p_prob, g + PER * j + half + 1)
                    for i in range(4):
                        mm = nc.tensor.transpose(att[:, half, i * P:(i + 1) * P], prob[:, j % 2, 4 * half + i, :],
                                                 ident[:, :])
                    mm.then_inc(s_probT, 1)

            def weigh_values(g, j):
                if j == 1:
                    pe.wait_ge(d_v, g + 3 * PER)
                else:
                    pe.wait_ge(d_v, g + (PER if j == 0 else UNIT))
                pe.wait_ge(d_probT, g + PER * (j + 1))
                for hh in range(NH):
                    p0 = (hh % HC) * HD
                    mm = nc.tensor.matmul(att[p0:p0 + HD, 3, (hh // HC) * P:(hh // HC + 1) * P],
                                          v[:, j, hh * HD:(hh + 1) * HD], probT[:, hh, :], start=True, stop=True,
                                          tile_position=(0, p0))
                mm.then_inc(s_oT, PER)

            def project_out(g, j, v_read):
                if v_read is not None:
                    pe.wait_ge(d_v, v_read)
                pe.wait_ge(d_oTlo, g + PER * (j + 1))
                for k in range(DC):
                    mm = split_product_rows(att[:, 2, D:2 * D], oT_hi[:, k, :], oT_lo[:, k, :], "wo", k,
                                            k == 0, k == DC - 1)
                mm.then_inc(s_proj, PER)

            def n2_transpose(gc, k, freed):
                if freed is not None:
                    pe.wait_ge(a_h, freed)
                if k == 0:
                    pe.wait_ge(d_n2, gc + UNIT)
                for j in range(GG):
                    mm = nc.tensor.transpose(step[:, k, j * P:(j + 1) * P], n2[:, j, k * P:(k + 1) * P], ident[:, :])
                mm.then_inc(s_n2T, HALF)

            def mlp_up(gc, c, projected=None):
                if c == 0:
                    pe.wait_ge(d_n2T, gc + UNIT)
                if projected is not None:
                    pe.wait_ge(a_qk, projected)
                elif c >= 2:
                    pe.wait_ge(a_h, gc + c - 1)
                for k in range(DC):
                    mm = split_product(step[:, c % 2, :], "w1", c * P, (c + 1) * P, n2T_hi[:, k, :], n2T_lo[:, k, :], k,
                                       k == 0, k == DC - 1)
                mm.then_inc(s_up, 1)

            def mlp_down(gc, c):
                if c == 0:
                    wait(pe, d_y, gc)
                pe.wait_ge(d_hlo, gc + c + 1)
                for j in range(GG):
                    mm = split_product_rows(mlp[:, j // 2, (j % 2) * D:(j % 2 + 1) * D],
                                            h_hi[:, c % HB, j * P:(j + 1) * P], h_lo[:, c % HB, j * P:(j + 1) * P],
                                            "w2", c, c == 0 and j % 2 == 0, c == FC - 1, skip=True)
                mm.then_inc(s_down, 1)

            pe.wait_ge(d_wlo, 3)
            for k in range(DC):
                nx_transpose(0, k)
            for m in range(2 * DC):
                project_qk(0, m)
            pe.wait_ge(d_wlo, 6)
            pe.wait_ge(d_bo, 1)

            def body(base, has):
                before, ahead, two_ago = base - UNIT, base + UNIT, base - 2 * UNIT

                def after_scores(j):
                    return base + PER * (j + 1) if has(0) else None

                if has(0):
                    scores(base, 0)
                if has(-2):
                    mlp_up(two_ago, 5, base + UNIT if has(0) else None)
                    mlp_up(two_ago, 6)
                if has(-1):
                    prob_transpose(before, 3, after_scores(0))
                if has(-2):
                    mlp_down(two_ago, 3)
                if has(-1):
                    weigh_values(before, 3)
                if has(0):
                    if not has(-1):
                        pe.wait_ge(d_score, base + PER)
                    project_v(base, 0)
                if has(-2):
                    mlp_down(two_ago, 4)
                if has(-1):
                    project_out(before, 3, base + PER if has(0) else None)
                if has(-2):
                    mlp_up(two_ago, 7)
                if has(0):
                    if not has(-1):
                        pe.wait_ge(d_v, base + PER)
                    scores(base, 1)
                if has(-2):
                    mlp_down(two_ago, 5)
                if has(-1):
                    for k in range(DC):
                        n2_transpose(before, k, base - 2 * UNIT + 7 + k if has(-2) else None)
                if has(0):
                    prob_transpose(base, 0, after_scores(1))
                if has(-2):
                    mlp_down(two_ago, 6)
                if has(0):
                    weigh_values(base, 0)
                    project_v(base, 1)
                if has(-2):
                    mlp_down(two_ago, 7)
                if has(0):
                    project_out(base, 0, base + 2 * PER)
                if has(-1):
                    mlp_up(before, 0)
                    mlp_up(before, 1)
                if has(0):
                    scores(base, 2)
                if has(-1):
                    mlp_up(before, 2)
                    mlp_up(before, 3)
                if has(0):
                    prob_transpose(base, 1, after_scores(2))
                    project_v(base, 3)
                if has(-1):
                    mlp_down(before, 0)
                if has(0):
                    weigh_values(base, 1)
                    project_v(base, 2)
                if has(-1):
                    mlp_down(before, 1)
                if has(1):
                    nx_transpose(ahead, 0, before + 3 if has(-1) else None)
                    nx_transpose(ahead, 1, before + 4 if has(-1) else None)
                if has(0):
                    project_out(base, 1, base + UNIT)
                if has(0):
                    scores(base, 3)
                if has(1):
                    project_qk(ahead, 0)
                    project_qk(ahead, 1)
                if has(0):
                    prob_transpose(base, 2, after_scores(3))
                if has(-1):
                    mlp_down(before, 2)
                if has(0):
                    weigh_values(base, 2)
                if has(1):
                    project_qk(ahead, 2)
                    project_qk(ahead, 3)
                if has(0):
                    project_out(base, 2, None)
                if has(-1):
                    mlp_up(before, 4, ahead + 3 * PER if has(1) else None)

            pipeline(pe, body)

        @block.scalar
        def _(act):
            act.wait_ge(dma_small, 160)
            act.wait_ge(dma_qkv, 48)
            for n in ("wq", "wk", "wv"):
                for k in range(DC):
                    w = act.activation(hi[n][:, k, :], raw[n][:, k, :], ACT.Identity, scale=ln_cols[:, 0, k:k + 1])
                w.then_inc(a_whi, 1)
            act.wait_ge(dma_rest, 48)
            act.copy(hi["wo"][:, :, :], raw["wo"][:, :, :]).then_inc(a_whi, 1)
            for k in range(DC):
                w = act.activation(hi["w1"][:, k, :], raw["w1"][:, k, :], ACT.Identity, scale=ln_cols[:, 2, k:k + 1])
            w.then_inc(a_whi, 1)
            act.copy(hi["w2"][:, :, :], raw["w2"][:, :, :]).then_inc(a_whi, 1)

            def nxT_high(ga, k):
                act.wait_ge(s_nxT, ga + HALF * (k + 1))
                act.copy(nxT_hi[:, k, :], step[:, k, :]).then_inc(a_nxT, HALF)

            def qk_out(ga, m):
                act.wait_ge(s_qk, ga + PER * (m + 1))
                c = m // 2
                if m % 2 == 0:
                    i = act.activation(qT[:, c, :], step[:, 0, :], ACT.Identity, bias=bq_scaled[:, c:c + 1], scale=SCALE)
                else:
                    i = act.activation(kT[:, c, :], step[:, 1, :], ACT.Identity, bias=bias_col[:, DC + c:DC + c + 1])
                i.then_inc(a_qk, PER)

            def n2T_high(gc, k):
                act.wait_ge(s_n2T, gc + HALF * (k + 1))
                act.copy(n2T_hi[:, k, :], step[:, k, :]).then_inc(a_n2T, HALF)

            def gelu(gc, c):
                act.wait_ge(s_up, gc + c + 1)
                if c >= 2:
                    act.wait_ge(d_hlo, gc + c - 1)
                act.activation(h[:, c % 2, :], step[:, c % 2, :], ACT.Gelu,
                               bias=bias_col[:, 3 * DC + c:3 * DC + c + 1]).then_inc(a_h, 1)

            def softmax(g, j):
                for half in range(2):
                    act.wait_ge(d_score, g + PER * j + half + 1)
                    for hh in range(4 * half, 4 * half + 4):
                        i = act.activation(prob[:, j % 2, hh, :], sneg[:, hh, :], ACT.Exp, bias=mneg[:, hh:hh + 1],
                                           scale=-1.0, accum_out=lsum[:, hh:hh + 1])
                    i.then_inc(a_prob, 1)

            def oT_high(g, j):
                act.wait_ge(s_oT, g + PER * (j + 1))
                act.copy(oT_hi[:, :, :], att[:, 3, 0:D].rearrange("p (c q) -> p c q", c=DC)).then_inc(a_oThi, PER)

            act.wait_ge(d_bcol, 2)
            for k in range(DC):
                nxT_high(0, k)
            for m in range(2 * DC):
                qk_out(0, m)

            def body(base, has):
                before, ahead, two_ago = base - UNIT, base + UNIT, base - 2 * UNIT
                if has(0):
                    softmax(base, 0)
                if has(-2):
                    gelu(two_ago, 5)
                if has(-1):
                    oT_high(before, 3)
                if has(-2):
                    gelu(two_ago, 6)
                    gelu(two_ago, 7)
                if has(0):
                    softmax(base, 1)
                if has(-1):
                    n2T_high(before, 0)
                    n2T_high(before, 1)
                if has(0):
                    oT_high(base, 0)
                if has(-1):
                    gelu(before, 0)
                    gelu(before, 1)
                if has(0):
                    softmax(base, 2)
                if has(-1):
                    gelu(before, 2)
                if has(0):
                    oT_high(base, 1)
                if has(-1):
                    gelu(before, 3)
                if has(1):
                    nxT_high(ahead, 0)
                    nxT_high(ahead, 1)
                if has(0):
                    softmax(base, 3)
                if has(1):
                    qk_out(ahead, 0)
                    qk_out(ahead, 1)
                if has(0):
                    oT_high(base, 2)
                if has(1):
                    qk_out(ahead, 2)
                    qk_out(ahead, 3)
                if has(-1):
                    gelu(before, 4)

            pipeline(act, body)

        @block.vector
        def _(dve):
            def low(out_, full, high):
                return dve.tensor_tensor(out_, full, high.bitcast(F32), ALU.subtract)

            def ln_stats(src, st, mv, js, d_st, d_mv, at, inc):
                for j in js:
                    i = dve.bn_stats(st[:, j, :], src[:, j, :])
                i.then_inc(d_st, inc)
                dve.wait_ge(d_st, at)
                dve.sem_inc(d_alone, 1)
                for j in js:
                    i = dve.bn_aggr(mv[:, j, :], st[:, j, :])
                i.then_inc(d_mv, inc)

            def ln1_stats(ga, half):
                dve.wait_ge(dma_x, 2 * ga + 16)
                ln_stats(x_in, st1, mv1, (2 * half, 2 * half + 1), d_st1, d_mv1, ga + HALF * (half + 1), HALF)

            def ln1_apply(ga):
                dve.wait_ge(p_rs1, ga + UNIT)
                for j in range(GG):
                    i = dve.tensor_scalar(nx[:, j, :], x_in[:, j, :], mv1[:, j, 0:1], rs1[:, j:j + 1],
                                          ALU.subtract, ALU.mult)
                i.then_inc(d_nx, UNIT)

            def nxT_low(ga, k):
                dve.wait_ge(a_nxT, ga + HALF * (k + 1))
                low(nxT_lo[:, k, :], step[:, k, :], nxT_hi[:, k, :]).then_inc(d_nxT, HALF)

            def v_out(g, j):
                dve.wait_ge(s_v, g + PER * ((0, 1, 3, 2)[j] + 1))
                dve.tensor_copy(v[:, j, :], att[:, 3 if j == 3 else 2, D:2 * D]).then_inc(d_v, PER)

            def edges(ga):
                dve.wait_ge(dma_adj, 2 * ga + 16)
                dve.tensor_scalar(adj_m[:, :, :], adj_in[:, :, :], 0.0, 1.0, ALU.is_gt, ALU.subtract).then_inc(d_adj, HALF)
                dve.scalar_tensor_tensor(out=adj_e[:, :, :], in0=adj_in[:, :, :], scalar=0.1, in1=adj_in[:, :, :],
                                         op0=ALU.mult, op1=ALU.mult).then_inc(d_adj, HALF)
                dve.wait_ge(d_adj, ga + UNIT)
                dve.scalar_tensor_tensor(out=edge_bias[:, :, :], in0=adj_m[:, :, :], scalar=MASKED, in1=adj_e[:, :, :],
                                         op0=ALU.mult, op1=ALU.add).then_inc(d_bias, UNIT)

            def score_max(g, j, half):
                if j == 0 and half == 0:
                    dve.wait_ge(d_bias, g + UNIT)
                dve.wait_ge(s_score, g + PER * (j + 1))
                dve.sem_inc(d_alone, 1)
                for hh in range(4 * half, 4 * half + 4):
                    i = dve.tensor_tensor_reduce(out=sneg[:, hh, :], in0=att[:, hh % 4, (hh // 4) * P:(hh // 4 + 1) * P],
                                                 in1=edge_bias[:, j, :], scale=-1.0, scalar=3e38, op0=ALU.add,
                                                 op1=ALU.min, accum_out=mneg[:, hh:hh + 1])
                i.then_inc(d_score, 1)

            def sums_inverse(g, j):
                dve.wait_ge(a_prob, g + PER * (j + 1))
                dve.reciprocal(rinv[:, :], lsum[:, :]).then_inc(d_rinv, PER)

            def probT_out(g, j):
                for half in range(2):
                    dve.wait_ge(s_probT, g + PER * j + half + 1)
                    dve.tensor_copy(probT[:, 4 * half:4 * half + 4, :],
                                    att[:, half, :].rearrange("p (h q) -> p h q", h=4)).then_inc(d_probT, 1)

            def oT_low(g, j):
                dve.wait_ge(a_oThi, g + PER * (j + 1))
                low(oT_lo[:, :, :], att[:, 3, 0:D].rearrange("p (c q) -> p c q", c=DC), oT_hi[:, :, :]).then_inc(d_oTlo, PER)

            def residual(g, j):
                dve.wait_ge(p_xbo, g + PER * (j + 1))
                wait(dve, p_x1b2, g - UNIT + PER * (j + 1))
                dve.wait_ge(s_proj, g + PER * (j + 1))
                dve.tensor_tensor(x1[:, j, :], att[:, 2, D:2 * D], x_bo[:, j, :], ALU.add).then_inc(d_x1, PER)

            def ln2_stats(g, j):
                dve.wait_ge(d_x1, g + PER * (j + 1))
                ln_stats(x1, st2, mv2, (j,), d_st2, d_mv2, g + PER * (j + 1), PER)

            def ln2_apply(g, j):
                dve.wait_ge(p_rs2, g + PER * (j + 1))
                dve.tensor_scalar(n2[:, j, :], x1[:, j, :], mv2[:, j, 0:1], rs2[:, j:j + 1], ALU.subtract,
                                  ALU.mult).then_inc(d_n2, PER)

            def n2T_low(gc, k):
                dve.wait_ge(a_n2T, gc + HALF * (k + 1))
                low(n2T_lo[:, k, :], step[:, k, :], n2T_hi[:, k, :]).then_inc(d_n2T, HALF)

            def h_split(gc, c):
                dve.wait_ge(a_h, gc + c + 1)
                if c >= HB:
                    dve.wait_ge(s_down, gc + c - HB + 1)
                dve.tensor_copy(h_hi[:, c % HB, :], h[:, c % 2, :]).then_inc(d_hhi, 1)
                dve.wait_ge(d_hhi, gc + c + 1)
                low(h_lo[:, c % HB, :], h[:, c % 2, :], h_hi[:, c % HB, :]).then_inc(d_hlo, 1)

            def y_out(gc, half):
                dve.wait_ge(s_down, gc + UNIT)
                if half == 0:
                    dve.wait_ge(p_x1b2, gc + UNIT)
                    wait(dve, dma_out, 2 * gc)
                resid = x1_b2[:, bass.ds(((gc // UNIT) % 2) * (GG * D) + half * 2 * D, 2 * D)]
                dve.tensor_tensor(y[:, 2 * half:2 * half + 2, :], mlp[:, half, :].rearrange("p (j d) -> p j d", j=2),
                                  resid.rearrange("p (j d) -> p j d", j=2), ALU.add).then_inc(d_y, HALF)

            ln1_stats(0, 0)
            ln1_stats(0, 1)
            dve.wait_ge(dma_small, 160)
            for m, n in enumerate(("wq", "wk", "wv")):
                dve.wait_ge(a_whi, m + 1)
                for k in range(DC):
                    i = dve.scalar_tensor_tensor(out=lo[n][:, k, :], in0=raw[n][:, k, :], scalar=ln_cols[:, 0, k:k + 1],
                                                 in1=hi[n][:, k, :].bitcast(F32), op0=ALU.mult, op1=ALU.subtract)
                i.then_inc(d_wlo, 1)
            ln1_apply(0)
            dve.wait_ge(s_bcol, 1)
            dve.tensor_tensor(bias_col[:, :], att[:, 0, 0:3 * DC + FC], bias_in[:, :], ALU.add).then_inc(d_bcol, 1)
            dve.wait_ge(d_bcol, 1)
            dve.tensor_scalar(bq_scaled[:, :], bias_col[:, 0:DC], SCALE, None, ALU.mult).then_inc(d_bcol, 1)
            dve.wait_ge(s_bo, 1)
            dve.tensor_tensor(bo_row[:, :], att[:, 1, 0:D], bo_row[:, :], ALU.add).then_inc(d_bo, 1)
            for k in range(DC):
                nxT_low(0, k)
            edges(0)
            dve.wait_ge(a_whi, 4)
            low(lo["wo"][:, :, :], raw["wo"][:, :, :], hi["wo"][:, :, :]).then_inc(d_wlo, 1)
            dve.wait_ge(a_whi, 6)
            for k in range(DC):
                i = dve.scalar_tensor_tensor(out=lo["w1"][:, k, :], in0=raw["w1"][:, k, :], scalar=ln_cols[:, 2, k:k + 1],
                                             in1=hi["w1"][:, k, :].bitcast(F32), op0=ALU.mult, op1=ALU.subtract)
            i.then_inc(d_wlo, 1)
            low(lo["w2"][:, :, :], raw["w2"][:, :, :], hi["w2"][:, :, :]).then_inc(d_wlo, 1)

            def body(base, has):
                before, ahead, two_ago = base - UNIT, base + UNIT, base - 2 * UNIT
                if has(0):
                    score_max(base, 0, 0)
                    score_max(base, 0, 1)
                if has(-2):
                    h_split(two_ago, 4)
                if has(-1):
                    probT_out(before, 3)
                if has(0):
                    sums_inverse(base, 0)
                if has(0):
                    v_out(base, 0)
                if has(-1):
                    oT_low(before, 3)
                if has(-2):
                    h_split(two_ago, 5)
                if has(-1):
                    residual(before, 3)
                    ln2_stats(before, 3)
                if has(-2):
                    h_split(two_ago, 6)
                if has(-1):
                    ln2_apply(before, 3)
                if has(0):
                    score_max(base, 1, 0)
                    score_max(base, 1, 1)
                if has(-2):
                    h_split(two_ago, 7)
                if has(0):
                    probT_out(base, 0)
                    sums_inverse(base, 1)
                if has(-1):
                    n2T_low(before, 0)
                if has(0):
                    oT_low(base, 0)
                    v_out(base, 1)
                if has(-1):
                    n2T_low(before, 1)
                if has(-2):
                    y_out(two_ago, 0)
                if has(0):
                    residual(base, 0)
                    ln2_stats(base, 0)
                if has(1):
                    ln1_stats(ahead, 0)
                    ln1_stats(ahead, 1)
                if has(0):
                    ln2_apply(base, 0)
                if has(-2):
                    y_out(two_ago, 1)
                if has(0):
                    score_max(base, 2, 0)
                    score_max(base, 2, 1)
                if has(-1):
                    h_split(before, 0)
                if has(0):
                    probT_out(base, 1)
                    v_out(base, 3)
                    sums_inverse(base, 2)
                if has(-1):
                    h_split(before, 1)
                if has(1):
                    ln1_apply(ahead)
                if has(0):
                    oT_low(base, 1)
                    v_out(base, 2)
                if has(1):
                    nxT_low(ahead, 0)
                if has(0):
                    residual(base, 1)
                if has(1):
                    nxT_low(ahead, 1)
                if has(0):
                    ln2_stats(base, 1)
                if has(0):
                    score_max(base, 3, 0)
                    score_max(base, 3, 1)
                    ln2_apply(base, 1)
                if has(-1):
                    h_split(before, 2)
                if has(0):
                    probT_out(base, 2)
                    sums_inverse(base, 3)
                    oT_low(base, 2)
                if has(-1):
                    h_split(before, 3)
                if has(0):
                    residual(base, 2)
                    ln2_stats(base, 2)
                if has(1):
                    edges(ahead)
                if has(0):
                    ln2_apply(base, 2)

            pipeline(dve, body)


_INS = ['x', 'adj'] + ['L0_gnn_' + n for n in ('ln1_g', 'ln1_b', 'ln2_g', 'ln2_b', 'wq', 'bq', 'wk', 'bk', 'wv', 'bv',
                                              'wo', 'bo', 'w1', 'b1', 'w2', 'b2')]
_OUTS = [((64, 128, 256), 'float32')]


def kernel(**inputs):
    import numpy as _np
    import concourse.bacc as _bacc
    from concourse import mybir as _mybir
    from concourse.bass_utils import run_bass_kernel_spmd as _run

    nc = _bacc.Bacc("TRN2", target_bir_lowering=False, num_devices=1)
    arrays, args = {}, []
    for name in _INS:
        a = _np.ascontiguousarray(inputs[name])
        arrays[f"in_{name}_dram"] = a
        args.append(nc.dram_tensor(f"in_{name}_dram", a.shape, _mybir.dt.from_np(a.dtype), kind="ExternalInput").ap())
    for i, (shape, dtype) in enumerate(_OUTS):
        dt = _mybir.dt.from_np(_np.dtype(dtype))
        args.append(nc.dram_tensor(f"out_{i}_dram", shape, dt, kind="ExternalOutput").ap())
    gnn_layer(nc, *args)
    r = _run(nc, [arrays], core_ids=[0])
    got = tuple(r.results[0][f"out_{i}_dram"] for i in range(len(_OUTS)))
    return got[0]
```

```python
from contextlib import ExitStack

import concourse.bass as bass
from concourse import mybir

ALU = mybir.AluOpType
ACT = mybir.ActivationFunctionType
F32 = mybir.dt.float32
F32R = mybir.dt.float32r
I32 = mybir.dt.int32

P = 128
D = 256
DC = D // P
NH = 8
HD = D // NH
HC = P // HD
FF = 4 * D
FC = FF // P
GG = 4
T = GG * P
HB = 4
EPS = 1e-5
SCALE = float(HD) ** -0.5
MASKED = 1e30
UNIT = 8


def gnn_layer(nc, x, adj, vec_cols, vec_rows, wq, wk, wv, wo, w1, w2, out):
    NG = x.shape[0] // GG
    xs = x.rearrange("b s d -> (b s) d")
    adjs = adj.rearrange("b s t -> (b s) t")
    outs = out.rearrange("b s d -> (b s) d")
    ROWS = T // UNIT

    with ExitStack() as ctx:
        def sb(name, shape, dt=F32):
            return ctx.enter_context(nc.sbuf_tensor(name, shape, dt))

        def sem(name):
            return ctx.enter_context(nc.semaphore(name))

        raw = {n: sb(f"{n}_raw", [P, s[0], s[1]]) for n, s in
               dict(wq=(DC, D), wk=(DC, D), wv=(DC, D), wo=(DC, D), w1=(DC, FF), w2=(FC, D)).items()}
        hi = {n: sb(f"{n}_hi", list(t.shape), F32R) for n, t in raw.items()}
        lo = {n: sb(f"{n}_lo", list(t.shape), F32R) for n, t in raw.items()}
        cols_in = sb("cols_in", [P, 4 * DC + 3 * DC + FC])
        bias_col = sb("bias_col", [P, 3 * DC + FC])
        bq_scaled = sb("bq_scaled", [P, DC])
        rows_in = sb("rows_in", [P, 2 * D])
        bo_row = sb("bo_row", [P, D])
        ident = sb("ident", [P, P])
        eps_t = sb("eps_t", [P, GG])
        mhalf = sb("mhalf", [P, GG])
        x_in = sb("x_in", [P, GG, D])
        adj_in = sb("adj_in", [P, GG, P], I32)
        adj_m = sb("adj_m", [P, GG, P])
        adj_e = sb("adj_e", [P, GG, P])
        edge_bias = sb("edge_bias", [P, GG, P])
        st1 = sb("st1", [P, GG, 6])
        mv1 = sb("mv1", [P, GG, 2])
        ve1 = sb("ve1", [P, GG])
        rs1 = sb("rs1", [P, GG])
        nx = sb("nx", [P, GG, D])
        nxT_hi = sb("nxT_hi", [P, DC, T], F32R)
        nxT_lo = sb("nxT_lo", [P, DC, T], F32R)
        qT = sb("qT", [P, DC, T])
        kT = sb("kT", [P, DC, T])
        v = sb("v", [P, GG, D])
        x_bo = sb("x_bo", [P, GG, D])
        sneg = sb("sneg", [P, NH, P])
        mneg = sb("mneg", [P, NH])
        prob = sb("prob", [P, 2, NH, P])
        lsum = sb("lsum", [P, NH])
        rinv = sb("rinv", [P, NH])
        probT = sb("probT", [P, NH, P])
        oT_hi = sb("oT_hi", [P, DC, P], F32R)
        oT_lo = sb("oT_lo", [P, DC, P], F32R)
        x1 = sb("x1", [P, GG, D])
        st2 = sb("st2", [P, GG, 6])
        mv2 = sb("mv2", [P, GG, 2])
        ve2 = sb("ve2", [P, GG])
        rs2 = sb("rs2", [P, GG])
        n2 = sb("n2", [P, GG, D])
        x1_b2 = sb("x1_b2", [P, 2 * GG * D])
        n2T_hi = sb("n2T_hi", [P, DC, T], F32R)
        n2T_lo = sb("n2T_lo", [P, DC, T], F32R)
        h = sb("h", [P, 2, T])
        h_hi = sb("h_hi", [P, HB, T], F32R)
        h_lo = sb("h_lo", [P, HB, T], F32R)
        y = sb("y", [P, GG, D])

        att = ctx.enter_context(nc.psum_tensor("att", [P, 4, 512], F32))
        step = ctx.enter_context(nc.psum_tensor("step", [P, 2, 512], F32))
        mlp = ctx.enter_context(nc.psum_tensor("mlp", [P, 2, 512], F32))

        dma_small, dma_qkv, dma_rest = sem("dma_small"), sem("dma_qkv"), sem("dma_rest")
        d_alone, sp_alone, p_alone = sem("d_alone"), sem("sp_alone"), sem("p_alone")
        dma_x, dma_adj, dma_out = sem("dma_x"), sem("dma_adj"), sem("dma_out")
        p_ident, p_const = sem("p_ident"), sem("p_const")
        a_whi, d_wlo = sem("a_whi"), sem("d_wlo")
        s_bcol, d_bcol, s_bo, d_bo = sem("s_bcol"), sem("d_bcol"), sem("s_bo"), sem("d_bo")
        s_b1, d_b1 = sem("s_b1"), sem("d_b1")
        d_st1, d_mv1, p_ve1, p_rs1, d_nx = sem("d_st1"), sem("d_mv1"), sem("p_ve1"), sem("p_rs1"), sem("d_nx")
        s_nxT, a_nxT, d_nxT = sem("s_nxT"), sem("a_nxT"), sem("d_nxT")
        s_qk, a_qk, s_v, d_v = sem("s_qk"), sem("a_qk"), sem("s_v"), sem("d_v")
        d_adj, d_bias, p_xbo = sem("d_adj"), sem("d_bias"), sem("p_xbo")
        s_score, d_score, a_prob = sem("s_score"), sem("d_score"), sem("a_prob")
        s_probT, d_probT = sem("s_probT"), sem("d_probT")
        d_rinv, p_prob = sem("d_rinv"), sem("p_prob")
        s_oT, a_oThi, d_oTlo = sem("s_oT"), sem("a_oThi"), sem("d_oTlo")
        s_proj, d_x1, d_st2, d_mv2 = sem("s_proj"), sem("d_x1"), sem("d_st2"), sem("d_mv2")
        p_ve2, p_rs2, d_n2, p_x1b2 = sem("p_ve2"), sem("p_rs2"), sem("d_n2"), sem("p_x1b2")
        s_n2T, a_n2T, d_n2T = sem("s_n2T"), sem("a_n2T"), sem("d_n2T")
        s_up, a_h, d_hhi, d_hlo, s_down, d_y = (sem("s_up"), sem("a_h"), sem("d_hhi"), sem("d_hlo"),
                                                sem("s_down"), sem("d_y"))

        PER = UNIT // GG
        HALF = UNIT // DC

        def ln_col(n, k):
            return cols_in[:, n * DC + k:n * DC + k + 1]

        def wait(eng, semaphore, value):
            if not isinstance(value, int) or value > 0:
                eng.wait_ge(semaphore, value)

        def split_product(psum, w, n_from, n_to, a_hi, a_lo, k, first, last):
            for t, (l, r) in enumerate(((lo[w], a_hi), (hi[w], a_lo), (hi[w], a_hi))):
                mm = nc.tensor.matmul(psum, l[:, k, n_from:n_to], r, start=first and t == 0, stop=last and t == 2)
            return mm

        def split_product_rows(psum, a_hi, a_lo, w, k, first, last, skip=False):
            for t, (l, r) in enumerate(((a_hi, lo[w]), (a_lo, hi[w]), (a_hi, hi[w]))):
                mm = nc.tensor.matmul(psum, l, r[:, k, :], start=first and t == 0, stop=last and t == 2,
                                      skip_group_check=skip)
            return mm

        block = ctx.enter_context(nc.Block())

        FIRST, LAST = 3, NG - 2

        def pipeline(eng, body):
            for i in range(FIRST):
                body(UNIT * i, lambda k: 0 <= i + k < NG)
            with eng.Fori(UNIT * FIRST, UNIT * LAST + 1, UNIT) as base:
                body(base, lambda k: True)
            for i in range(LAST + 1, NG + 2):
                body(UNIT * i, lambda k: 0 <= i + k < NG)

        @block.sync
        def _(sp):
            def load_x(g):
                sp.dma_start(x_in[:, :, :], xs[bass.ds(g * ROWS, T), :].rearrange("(j p) d -> p j d", p=P)).then_inc(dma_x, 16)

            def load_adj(g):
                sp.dma_start(adj_in[:, :, :], adjs[bass.ds(g * ROWS, T), :].rearrange("(j p) d -> p j d", p=P)).then_inc(dma_adj, 16)

            load_x(0)
            sp.dma_start(cols_in[:, :], vec_cols[:, :]).then_inc(dma_small, 16)
            sp.dma_start(rows_in[:, :], vec_rows.rearrange("(a d) -> a d", a=1).to_broadcast([P, 2 * D])).then_inc(dma_small, 16)
            load_adj(0)

            def body(base, has):
                if has(1):
                    sp.wait_ge(d_nx, base + UNIT)
                    sp.wait_ge(p_xbo, base + UNIT)
                    sp.sem_inc(sp_alone, 1)
                    load_x(base + UNIT)
                    sp.wait_ge(d_bias, base + UNIT)
                    sp.sem_inc(sp_alone, 1)
                    load_adj(base + UNIT)
                if has(-2):
                    sp.wait_ge(d_y, base - UNIT)
                    sp.sem_inc(sp_alone, 1)
                    sp.dma_start(outs[bass.ds((base - 2 * UNIT) * ROWS, T), :].rearrange("(j p) d -> p j d", p=P),
                                 y[:, :, :]).then_inc(dma_out, 16)

            pipeline(sp, body)
            sp.wait_ge(dma_out, 16 * NG)

        @block.gpsimd
        def _(pool):
            pool.memset(ident[:, :], 0.0).then_inc(p_const, 1)
            pool.memset(eps_t[:, :], EPS).then_inc(p_const, 1)
            pool.memset(mhalf[:, :], -0.5).then_inc(p_const, 1)
            pool.wait_ge(p_const, 3)
            pool.affine_select(out=ident[:, :], in_=ident[:, :], compare_op=ALU.not_equal, fill=1.0, base=0,
                               pattern=[[-1, P]], channel_multiplier=1).then_inc(p_ident, 1)

            def rstd(mv, ve, rs, js, d_mv, p_ve, p_rs, at, inc):
                j0, j1 = js
                pool.wait_ge(d_mv, at)
                pool.tensor_tensor(ve[:, j0:j1], mv[:, j0:j1, 1], eps_t[:, j0:j1], ALU.add).then_inc(p_ve, inc)
                pool.wait_ge(p_ve, at)
                pool.tensor_tensor(rs[:, j0:j1], ve[:, j0:j1], mhalf[:, j0:j1], ALU.pow).then_inc(p_rs, inc)

            def add_bo(ga, j):
                wait(pool, d_x1, ga - UNIT + PER * (j + 1))
                pool.wait_ge(dma_x, 2 * ga + 16)
                pool.tensor_tensor(x_bo[:, j, :], x_in[:, j, :], bo_row[:, :], ALU.add).then_inc(p_xbo, PER)

            def add_b2(g, j):
                pool.wait_ge(d_x1, g + PER * (j + 1))
                wait(pool, d_y, g - UNIT)
                pool.sem_inc(p_alone, 1)
                pool.tensor_tensor(x1_b2[:, bass.ds(((g // UNIT) % 2) * (GG * D) + j * D, D)], x1[:, j, :],
                                   rows_in[:, D:2 * D], ALU.add).then_inc(p_x1b2, PER)

            def scale_prob(g, j):
                pool.wait_ge(d_rinv, g + PER * (j + 1))
                for half in range(2):
                    heads = slice(4 * half, 4 * half + 4)
                    pool.tensor_tensor(prob[:, j % 2, heads, :], prob[:, j % 2, heads, :],
                                       rinv[:, heads].unsqueeze(2).to_broadcast([P, 4, P]), ALU.mult).then_inc(p_prob, 1)

            def rstd2(g, j):
                rstd(mv2, ve2, rs2, (j, j + 1), d_mv2, p_ve2, p_rs2, g + PER * (j + 1), PER)

            rstd(mv1, ve1, rs1, (0, GG), d_mv1, p_ve1, p_rs1, UNIT, UNIT)

            def body(base, has):
                if has(0):
                    scale_prob(base, 0)
                if has(0) and not has(-1):
                    pool.wait_ge(d_bo, 1)
                    for j in range(GG):
                        add_bo(0, j)
                if has(-1):
                    rstd2(base - UNIT, 3)
                    if has(0):
                        add_bo(base, 3)
                    add_b2(base - UNIT, 3)
                if has(0):
                    scale_prob(base, 1)
                    rstd2(base, 0)
                if has(1):
                    rstd(mv1, ve1, rs1, (0, GG), d_mv1, p_ve1, p_rs1, base + 2 * UNIT, UNIT)
                    add_bo(base + UNIT, 0)
                if has(0):
                    scale_prob(base, 2)
                    rstd2(base, 1)
                    add_b2(base, 0)
                    add_b2(base, 1)
                if has(1):
                    add_bo(base + UNIT, 1)
                if has(0):
                    scale_prob(base, 3)
                    rstd2(base, 2)
                    add_b2(base, 2)
                if has(1):
                    add_bo(base + UNIT, 2)

            pipeline(pool, body)

        @block.tensor
        def _(pe):
            def bias_behind(psum, n, ln_b, m0, m1):
                for m in range(m0, m1):
                    for k in range(DC):
                        mm = nc.tensor.matmul(psum[:, m:m + 1], raw[n][:, k, m * P:(m + 1) * P], ln_col(ln_b, k),
                                              start=(k == 0), stop=(k == DC - 1))
                return mm

            def mlp_bias(m0, m1):
                mm = bias_behind(mlp[:, 1, D:D + FC], "w1", 3, m0, m1)
                if m1 == FC:
                    mm.then_inc(s_b1, 1)

            def nx_transpose(ga, k, freed=None):
                if freed is not None:
                    pe.wait_ge(a_h, freed)
                if k == 0:
                    pe.wait_ge(d_nx, ga + UNIT)
                for j in range(GG):
                    mm = nc.tensor.transpose(step[:, k, j * P:(j + 1) * P], nx[:, j, k * P:(k + 1) * P], ident[:, :])
                mm.then_inc(s_nxT, HALF)

            def project_qk(ga, m):
                if m == 0:
                    pe.wait_ge(d_nxT, ga + UNIT)
                if m >= 2:
                    pe.wait_ge(a_qk, ga + PER * (m - 1))
                w, c0 = ("wq", "wk")[m % 2], (m // 2) * P
                for k in range(DC):
                    mm = split_product(step[:, m % 2, :], w, c0, c0 + P, nxT_hi[:, k, :], nxT_lo[:, k, :], k,
                                       k == 0, k == DC - 1)
                mm.then_inc(s_qk, PER)

            def project_v(g, j):
                to = att[:, 3 if j == 3 else 2, D:2 * D]
                for k in range(DC):
                    mm = split_product_rows(to, nxT_hi[:, k, j * P:(j + 1) * P],
                                            nxT_lo[:, k, j * P:(j + 1) * P], "wv", k, k == 0, k == DC - 1)
                mm.then_inc(s_v, PER)

            def scores(g, j):
                wait(pe, d_oTlo, g + PER * (j - 1))
                for hh in (0, 1, 3, 4, 5, 7, 2, 6):
                    if j == 0 and hh in (0, 4):
                        pe.wait_ge(a_qk, g + 2 * PER * (hh // HC + 1))
                    if hh == 2:
                        wait(pe, d_x1, g + PER * (j - 1))
                    r0 = (hh % HC) * HD
                    mm = nc.tensor.matmul(att[:, hh % 4, (hh // 4) * P:(hh // 4 + 1) * P],
                                          qT[r0:r0 + HD, hh // HC, j * P:(j + 1) * P],
                                          kT[r0:r0 + HD, hh // HC, j * P:(j + 1) * P], start=True, stop=True,
                                          tile_position=(r0, 0))
                mm.then_inc(s_score, PER)

            def prob_transpose(g, j, others):
                if others is not None:
                    pe.wait_ge(d_score, others)
                else:
                    pe.wait_ge(d_x1, g + PER * j)
                for half in range(2):
                    pe.wait_ge(p_prob, g + PER * j + half + 1)
                    for i in range(4):
                        mm = nc.tensor.transpose(att[:, half, i * P:(i + 1) * P], prob[:, j % 2, 4 * half + i, :],
                                                 ident[:, :])
                    mm.then_inc(s_probT, 1)

            def weigh_values(g, j):
                if j == 1:
                    pe.wait_ge(d_v, g + 3 * PER)
                else:
                    pe.wait_ge(d_v, g + (PER if j == 0 else UNIT))
                pe.wait_ge(d_probT, g + PER * (j + 1))
                for hh in range(NH):
                    p0 = (hh % HC) * HD
                    mm = nc.tensor.matmul(att[p0:p0 + HD, 3, (hh // HC) * P:(hh // HC + 1) * P],
                                          v[:, j, hh * HD:(hh + 1) * HD], probT[:, hh, :], start=True, stop=True,
                                          tile_position=(0, p0))
                mm.then_inc(s_oT, PER)

            def project_out(g, j, v_read):
                if v_read is not None:
                    pe.wait_ge(d_v, v_read)
                pe.wait_ge(d_oTlo, g + PER * (j + 1))
                for k in range(DC):
                    mm = split_product_rows(att[:, 2, D:2 * D], oT_hi[:, k, :], oT_lo[:, k, :], "wo", k,
                                            k == 0, k == DC - 1)
                mm.then_inc(s_proj, PER)

            def n2_transpose(gc, k, freed):
                if freed is not None:
                    pe.wait_ge(a_h, freed)
                if k == 0:
                    pe.wait_ge(d_n2, gc + UNIT)
                for j in range(GG):
                    mm = nc.tensor.transpose(step[:, k, j * P:(j + 1) * P], n2[:, j, k * P:(k + 1) * P], ident[:, :])
                mm.then_inc(s_n2T, HALF)

            def mlp_up(gc, c, projected=None):
                if c == 0:
                    pe.wait_ge(d_n2T, gc + UNIT)
                if projected is not None:
                    pe.wait_ge(a_qk, projected)
                elif c >= 2:
                    pe.wait_ge(a_h, gc + c - 1)
                for k in range(DC):
                    mm = split_product(step[:, c % 2, :], "w1", c * P, (c + 1) * P, n2T_hi[:, k, :], n2T_lo[:, k, :], k,
                                       k == 0, k == DC - 1)
                mm.then_inc(s_up, 1)

            def mlp_down(gc, c):
                if c == 0:
                    wait(pe, d_y, gc)
                pe.wait_ge(d_hlo, gc + c + 1)
                for j in range(GG):
                    mm = split_product_rows(mlp[:, j // 2, (j % 2) * D:(j % 2 + 1) * D],
                                            h_hi[:, c % HB, j * P:(j + 1) * P], h_lo[:, c % HB, j * P:(j + 1) * P],
                                            "w2", c, c == 0 and j % 2 == 0, c == FC - 1, skip=True)
                mm.then_inc(s_down, 1)

            pe.wait_ge(p_ident, 1)
            for k in range(DC):
                nx_transpose(0, k)
            pe.wait_ge(dma_small, 32)
            pe.wait_ge(dma_qkv, 48)
            for m in range(2 * DC):
                if m < 2:
                    bias_behind(mlp[:, m, 0:DC], ("wq", "wk")[m], 1, 0, DC).then_inc(s_bcol, 1)
                    pe.wait_ge(d_wlo, m + 1)
                project_qk(0, m)
            pe.wait_ge(d_wlo, 3)
            pe.wait_ge(d_bcol, 3)
            for j in range(GG):
                for k in range(DC):
                    mm = split_product_rows(mlp[:, j // 2, (j % 2) * D:(j % 2 + 1) * D], nxT_hi[:, k, j * P:(j + 1) * P],
                                            nxT_lo[:, k, j * P:(j + 1) * P], "wv", k, k == 0, k == DC - 1)
                if j % 2 == 1:
                    mm.then_inc(s_v, HALF)

            def value_bias():
                pe.wait_ge(d_v, UNIT)
                bias_behind(mlp[:, 0, 0:DC], "wv", 1, 0, DC).then_inc(s_bcol, 1)
                pe.wait_ge(dma_rest, 48)
                mlp_bias(0, 2)

            def output_bias():
                pe.wait_ge(d_bcol, 4)
                for k in range(DC):
                    mm = nc.tensor.matmul(mlp[:, 1, 0:D], bias_col[:, 2 * DC + k:2 * DC + k + 1].to_broadcast([P, P]),
                                          raw["wo"][:, k, :], start=(k == 0), stop=(k == DC - 1))
                mm.then_inc(s_bo, 1)

            def body(base, has):
                before, ahead, two_ago = base - UNIT, base + UNIT, base - 2 * UNIT

                def after_scores(j):
                    return base + PER * (j + 1) if has(0) else None

                if has(0):
                    scores(base, 0)
                if has(0) and not has(-1):
                    value_bias()
                    pe.wait_ge(d_score, PER)
                if has(-2):
                    mlp_up(two_ago, 5, base + UNIT if has(0) else None)
                    mlp_up(two_ago, 6)
                if has(-1):
                    prob_transpose(before, 3, after_scores(0))
                if has(-2):
                    mlp_down(two_ago, 3)
                if has(0) and has(-1) and not has(-2):
                    project_v(base, 0)
                if has(-1):
                    weigh_values(before, 3)
                if has(0) and has(-2):
                    project_v(base, 0)
                if has(-2):
                    mlp_down(two_ago, 4)
                if has(-1):
                    project_out(before, 3, base + PER if has(0) else None)
                if has(-2):
                    mlp_up(two_ago, 7)
                if has(0):
                    scores(base, 1)
                if has(0) and not has(-1):
                    output_bias()
                if has(-2):
                    mlp_down(two_ago, 5)
                if has(-1):
                    for k in range(DC):
                        n2_transpose(before, k, base - 2 * UNIT + 7 + k if has(-2) else None)
                if has(0):
                    prob_transpose(base, 0, after_scores(1))
                    if not has(-1):
                        pe.wait_ge(d_bo, 1)
                        mlp_bias(2, 4)
                if has(-2):
                    mlp_down(two_ago, 6)
                if has(0) and has(-1) and not has(-2):
                    project_v(base, 1)
                if has(0):
                    weigh_values(base, 0)
                    if not has(-1):
                        mlp_bias(4, 6)
                if has(0) and has(-2):
                    project_v(base, 1)
                if has(-2):
                    mlp_down(two_ago, 7)
                if has(0):
                    if not has(-1):
                        pe.wait_ge(d_wlo, 4)
                    project_out(base, 0, base + 2 * PER)
                if has(-1):
                    if not has(-2):
                        pe.wait_ge(d_wlo, 5)
                    mlp_up(before, 0)
                    mlp_up(before, 1)
                if has(0):
                    scores(base, 2)
                    if not has(-1):
                        mlp_bias(6, FC)
                if has(-1):
                    mlp_up(before, 2)
                    mlp_up(before, 3)
                if has(0):
                    prob_transpose(base, 1, after_scores(2))
                if has(0) and has(-1):
                    project_v(base, 3)
                if has(-1):
                    if not has(-2):
                        pe.wait_ge(d_wlo, 6)
                    mlp_down(before, 0)
                if has(0):
                    weigh_values(base, 1)
                if has(0) and has(-1):
                    project_v(base, 2)
                if has(-1):
                    mlp_down(before, 1)
                if has(1):
                    nx_transpose(ahead, 0, before + 3 if has(-1) else None)
                    nx_transpose(ahead, 1, before + 4 if has(-1) else None)
                if has(0):
                    project_out(base, 1, base + UNIT)
                if has(0):
                    scores(base, 3)
                if has(1):
                    project_qk(ahead, 0)
                    project_qk(ahead, 1)
                elif has(-1):
                    mlp_up(before, 4)
                if has(0):
                    prob_transpose(base, 2, after_scores(3))
                if has(-1):
                    mlp_down(before, 2)
                if has(0):
                    weigh_values(base, 2)
                if has(1):
                    project_qk(ahead, 2)
                    project_qk(ahead, 3)
                if has(0):
                    project_out(base, 2, None)
                if has(-1) and has(1):
                    mlp_up(before, 4, ahead + 3 * PER)

            pipeline(pe, body)

        @block.scalar
        def _(act):
            for n, w in (("wq", wq), ("wk", wk), ("wv", wv)):
                act.dma_start(raw[n][:, :, :], w.rearrange("(k p) n -> p k n", p=P)).then_inc(dma_qkv, 16)
            for n, w in (("wo", wo), ("w1", w1), ("w2", w2)):
                act.dma_start(raw[n][:, :, :], w.rearrange("(k p) n -> p k n", p=P)).then_inc(dma_rest, 16)

            def weight_high(n, gain):
                if gain is None:
                    w = act.copy(hi[n][:, :, :], raw[n][:, :, :])
                else:
                    for k in range(DC):
                        w = act.activation(hi[n][:, k, :], raw[n][:, k, :], ACT.Identity, scale=ln_col(gain, k))
                w.then_inc(a_whi, 1)

            def nxT_high(ga, k):
                act.wait_ge(s_nxT, ga + HALF * (k + 1))
                act.copy(nxT_hi[:, k, :], step[:, k, :]).then_inc(a_nxT, HALF)

            def qk_out(ga, m):
                act.wait_ge(s_qk, ga + PER * (m + 1))
                c = m // 2
                if m % 2 == 0:
                    i = act.activation(qT[:, c, :], step[:, 0, :], ACT.Identity, bias=bq_scaled[:, c:c + 1], scale=SCALE)
                else:
                    i = act.activation(kT[:, c, :], step[:, 1, :], ACT.Identity, bias=bias_col[:, DC + c:DC + c + 1])
                i.then_inc(a_qk, PER)

            def n2T_high(gc, k):
                act.wait_ge(s_n2T, gc + HALF * (k + 1))
                act.copy(n2T_hi[:, k, :], step[:, k, :]).then_inc(a_n2T, HALF)

            def gelu(gc, c):
                act.wait_ge(s_up, gc + c + 1)
                if c >= 2:
                    act.wait_ge(d_hlo, gc + c - 1)
                act.activation(h[:, c % 2, :], step[:, c % 2, :], ACT.Gelu,
                               bias=bias_col[:, 3 * DC + c:3 * DC + c + 1]).then_inc(a_h, 1)

            def softmax(g, j):
                for half in range(2):
                    act.wait_ge(d_score, g + PER * j + half + 1)
                    for hh in range(4 * half, 4 * half + 4):
                        i = act.activation(prob[:, j % 2, hh, :], sneg[:, hh, :], ACT.Exp, bias=mneg[:, hh:hh + 1],
                                           scale=-1.0, accum_out=lsum[:, hh:hh + 1])
                    i.then_inc(a_prob, 1)

            def oT_high(g, j):
                act.wait_ge(s_oT, g + PER * (j + 1))
                act.copy(oT_hi[:, :, :], att[:, 3, 0:D].rearrange("p (c q) -> p c q", c=DC)).then_inc(a_oThi, PER)

            act.wait_ge(dma_small, 32)
            act.wait_ge(dma_qkv, 48)
            weight_high("wq", 0)
            for k in range(DC):
                nxT_high(0, k)
            weight_high("wk", 0)
            weight_high("wv", 0)
            act.wait_ge(dma_rest, 48)
            weight_high("wo", None)
            weight_high("w1", 2)
            act.wait_ge(d_bcol, 3)
            for m in range(2 * DC):
                qk_out(0, m)
            weight_high("w2", None)

            def body(base, has):
                before, ahead, two_ago = base - UNIT, base + UNIT, base - 2 * UNIT
                if has(0):
                    softmax(base, 0)
                if has(-2):
                    gelu(two_ago, 5)
                if has(-1):
                    oT_high(before, 3)
                if has(-2):
                    gelu(two_ago, 6)
                    gelu(two_ago, 7)
                if has(0):
                    softmax(base, 1)
                if has(-1):
                    n2T_high(before, 0)
                    n2T_high(before, 1)
                if has(0):
                    oT_high(base, 0)
                if has(-1):
                    if not has(-2):
                        act.wait_ge(d_b1, 1)
                    gelu(before, 0)
                    gelu(before, 1)
                if has(0):
                    softmax(base, 2)
                if has(-1):
                    gelu(before, 2)
                if has(0):
                    oT_high(base, 1)
                if has(-1):
                    gelu(before, 3)
                if has(1):
                    nxT_high(ahead, 0)
                    nxT_high(ahead, 1)
                if has(0):
                    softmax(base, 3)
                if has(1):
                    qk_out(ahead, 0)
                    qk_out(ahead, 1)
                if has(0):
                    oT_high(base, 2)
                if has(1):
                    qk_out(ahead, 2)
                    qk_out(ahead, 3)
                if has(-1):
                    gelu(before, 4)

            pipeline(act, body)

        @block.vector
        def _(dve):
            def low(out_, full, high):
                return dve.tensor_tensor(out_, full, high.bitcast(F32), ALU.subtract)

            def ln_stats(src, st, mv, js, d_st, d_mv, at, inc):
                for j in js:
                    i = dve.bn_stats(st[:, j, :], src[:, j, :])
                i.then_inc(d_st, inc)
                dve.wait_ge(d_st, at)
                dve.sem_inc(d_alone, 1)
                for j in js:
                    i = dve.bn_aggr(mv[:, j, :], st[:, j, :])
                i.then_inc(d_mv, inc)

            def ln1_stats(ga, half):
                dve.wait_ge(dma_x, 2 * ga + 16)
                ln_stats(x_in, st1, mv1, (2 * half, 2 * half + 1), d_st1, d_mv1, ga + HALF * (half + 1), HALF)

            def ln1_apply(ga):
                dve.wait_ge(p_rs1, ga + UNIT)
                for j in range(GG):
                    i = dve.tensor_scalar(nx[:, j, :], x_in[:, j, :], mv1[:, j, 0:1], rs1[:, j:j + 1],
                                          ALU.subtract, ALU.mult)
                i.then_inc(d_nx, UNIT)

            def nxT_low(ga, k):
                dve.wait_ge(a_nxT, ga + HALF * (k + 1))
                low(nxT_lo[:, k, :], step[:, k, :], nxT_hi[:, k, :]).then_inc(d_nxT, HALF)

            def v_out(g, j):
                dve.wait_ge(s_v, g + PER * ((0, 1, 3, 2)[j] + 1))
                dve.tensor_copy(v[:, j, :], att[:, 3 if j == 3 else 2, D:2 * D]).then_inc(d_v, PER)

            def edges(ga):
                dve.wait_ge(dma_adj, 2 * ga + 16)
                dve.tensor_scalar(adj_m[:, :, :], adj_in[:, :, :], 0.0, 1.0, ALU.is_gt, ALU.subtract).then_inc(d_adj, HALF)
                dve.scalar_tensor_tensor(out=adj_e[:, :, :], in0=adj_in[:, :, :], scalar=0.1, in1=adj_in[:, :, :],
                                         op0=ALU.mult, op1=ALU.mult).then_inc(d_adj, HALF)

            def edges_end(ga):
                dve.wait_ge(d_adj, ga + UNIT)
                dve.scalar_tensor_tensor(out=edge_bias[:, :, :], in0=adj_m[:, :, :], scalar=MASKED, in1=adj_e[:, :, :],
                                         op0=ALU.mult, op1=ALU.add).then_inc(d_bias, UNIT)

            def score_max(g, j, half):
                if j == 0 and half == 0:
                    dve.wait_ge(d_bias, g + UNIT)
                dve.wait_ge(s_score, g + PER * (j + 1))
                dve.sem_inc(d_alone, 1)
                for hh in range(4 * half, 4 * half + 4):
                    i = dve.tensor_tensor_reduce(out=sneg[:, hh, :], in0=att[:, hh % 4, (hh // 4) * P:(hh // 4 + 1) * P],
                                                 in1=edge_bias[:, j, :], scale=-1.0, scalar=3e38, op0=ALU.add,
                                                 op1=ALU.min, accum_out=mneg[:, hh:hh + 1])
                i.then_inc(d_score, 1)

            def sums_inverse(g, j):
                dve.wait_ge(a_prob, g + PER * (j + 1))
                dve.reciprocal(rinv[:, :], lsum[:, :]).then_inc(d_rinv, PER)

            def probT_out(g, j):
                for half in range(2):
                    dve.wait_ge(s_probT, g + PER * j + half + 1)
                    dve.tensor_copy(probT[:, 4 * half:4 * half + 4, :],
                                    att[:, half, :].rearrange("p (h q) -> p h q", h=4)).then_inc(d_probT, 1)

            def oT_low(g, j):
                dve.wait_ge(a_oThi, g + PER * (j + 1))
                low(oT_lo[:, :, :], att[:, 3, 0:D].rearrange("p (c q) -> p c q", c=DC), oT_hi[:, :, :]).then_inc(d_oTlo, PER)

            def residual(g, j):
                dve.wait_ge(p_xbo, g + PER * (j + 1))
                wait(dve, p_x1b2, g - UNIT + PER * (j + 1))
                dve.wait_ge(s_proj, g + PER * (j + 1))
                dve.tensor_tensor(x1[:, j, :], att[:, 2, D:2 * D], x_bo[:, j, :], ALU.add).then_inc(d_x1, PER)

            def ln2_stats(g, j):
                dve.wait_ge(d_x1, g + PER * (j + 1))
                ln_stats(x1, st2, mv2, (j,), d_st2, d_mv2, g + PER * (j + 1), PER)

            def ln2_apply(g, j):
                dve.wait_ge(p_rs2, g + PER * (j + 1))
                dve.tensor_scalar(n2[:, j, :], x1[:, j, :], mv2[:, j, 0:1], rs2[:, j:j + 1], ALU.subtract,
                                  ALU.mult).then_inc(d_n2, PER)

            def n2T_low(gc, k):
                dve.wait_ge(a_n2T, gc + HALF * (k + 1))
                low(n2T_lo[:, k, :], step[:, k, :], n2T_hi[:, k, :]).then_inc(d_n2T, HALF)

            def h_split(gc, c):
                dve.wait_ge(a_h, gc + c + 1)
                if c >= HB:
                    dve.wait_ge(s_down, gc + c - HB + 1)
                dve.tensor_copy(h_hi[:, c % HB, :], h[:, c % 2, :]).then_inc(d_hhi, 1)
                dve.wait_ge(d_hhi, gc + c + 1)
                low(h_lo[:, c % HB, :], h[:, c % 2, :], h_hi[:, c % HB, :]).then_inc(d_hlo, 1)

            def y_out(gc, half):
                dve.wait_ge(s_down, gc + UNIT)
                if half == 0:
                    dve.wait_ge(p_x1b2, gc + UNIT)
                    wait(dve, dma_out, 2 * gc)
                resid = x1_b2[:, bass.ds(((gc // UNIT) % 2) * (GG * D) + half * 2 * D, 2 * D)]
                dve.tensor_tensor(y[:, 2 * half:2 * half + 2, :], mlp[:, half, :].rearrange("p (j d) -> p j d", j=2),
                                  resid.rearrange("p (j d) -> p j d", j=2), ALU.add).then_inc(d_y, HALF)

            def weight_low(n, nth, gain):
                dve.wait_ge(a_whi, nth)
                if gain is None:
                    i = low(lo[n][:, :, :], raw[n][:, :, :], hi[n][:, :, :])
                else:
                    for k in range(DC):
                        i = dve.scalar_tensor_tensor(out=lo[n][:, k, :], in0=raw[n][:, k, :],
                                                     scalar=ln_col(gain, k), in1=hi[n][:, k, :].bitcast(F32),
                                                     op0=ALU.mult, op1=ALU.subtract)
                i.then_inc(d_wlo, 1)

            ln1_stats(0, 0)
            ln1_stats(0, 1)
            ln1_apply(0)
            dve.wait_ge(dma_small, 32)
            weight_low("wq", 1, 0)
            for k in range(DC):
                nxT_low(0, k)
            def bias_column(nth):
                c0 = nth * DC
                dve.wait_ge(s_bcol, nth + 1)
                dve.tensor_tensor(bias_col[:, c0:c0 + DC], mlp[:, nth % 2, 0:DC], cols_in[:, 4 * DC + c0:5 * DC + c0],
                                  ALU.add).then_inc(d_bcol, 1)

            bias_column(0)
            dve.wait_ge(d_bcol, 1)
            dve.tensor_scalar(bq_scaled[:, :], bias_col[:, 0:DC], SCALE, None, ALU.mult).then_inc(d_bcol, 1)
            weight_low("wk", 2, 0)
            bias_column(1)
            weight_low("wv", 3, 0)
            edges(0)
            edges_end(0)
            weight_low("wo", 4, None)
            weight_low("w1", 5, 2)
            for half in range(2):
                dve.wait_ge(s_v, HALF * (half + 1))
                dve.tensor_copy(v[:, 2 * half:2 * half + 2, :],
                                mlp[:, half, :].rearrange("p (j d) -> p j d", j=2)).then_inc(d_v, HALF)

            def body(base, has):
                before, ahead, two_ago = base - UNIT, base + UNIT, base - 2 * UNIT
                if has(0):
                    score_max(base, 0, 0)
                    score_max(base, 0, 1)
                if has(0) and not has(-1):
                    bias_column(2)
                    weight_low("w2", 6, None)
                if has(-2):
                    h_split(two_ago, 4)
                if has(-1):
                    probT_out(before, 3)
                if has(0):
                    sums_inverse(base, 0)
                if has(-1):
                    if has(0):
                        v_out(base, 0)
                    oT_low(before, 3)
                if has(-2):
                    h_split(two_ago, 5)
                if has(-1):
                    residual(before, 3)
                    ln2_stats(before, 3)
                if has(-2):
                    h_split(two_ago, 6)
                if has(-1):
                    ln2_apply(before, 3)
                if has(0):
                    score_max(base, 1, 0)
                    score_max(base, 1, 1)
                if has(0) and not has(-1):
                    dve.wait_ge(s_bo, 1)
                    dve.tensor_tensor(bo_row[:, :], mlp[:, 1, 0:D], rows_in[:, 0:D], ALU.add).then_inc(d_bo, 1)
                if has(-2):
                    h_split(two_ago, 7)
                if has(0):
                    probT_out(base, 0)
                    sums_inverse(base, 1)
                if has(-1):
                    n2T_low(before, 0)
                if has(0):
                    oT_low(base, 0)
                    if has(-1):
                        v_out(base, 1)
                if has(-1):
                    n2T_low(before, 1)
                if has(-2):
                    y_out(two_ago, 0)
                if has(0):
                    residual(base, 0)
                    ln2_stats(base, 0)
                if has(1):
                    ln1_stats(ahead, 0)
                    ln1_stats(ahead, 1)
                if has(0):
                    ln2_apply(base, 0)
                if has(-2):
                    y_out(two_ago, 1)
                if has(0):
                    score_max(base, 2, 0)
                    score_max(base, 2, 1)
                if has(-1):
                    h_split(before, 0)
                if has(0):
                    probT_out(base, 1)
                    if has(-1):
                        v_out(base, 3)
                    sums_inverse(base, 2)
                if has(-1):
                    h_split(before, 1)
                if has(1):
                    ln1_apply(ahead)
                if has(0):
                    oT_low(base, 1)
                    if has(-1):
                        v_out(base, 2)
                if has(1):
                    nxT_low(ahead, 0)
                if has(0):
                    residual(base, 1)
                if has(1):
                    nxT_low(ahead, 1)
                if has(0):
                    ln2_stats(base, 1)
                if has(0):
                    score_max(base, 3, 0)
                    score_max(base, 3, 1)
                    ln2_apply(base, 1)
                if has(0) and not has(-1):
                    dve.wait_ge(s_b1, 1)
                    dve.tensor_tensor(bias_col[:, 3 * DC:], mlp[:, 1, D:D + FC], cols_in[:, 7 * DC:], ALU.add).then_inc(d_b1, 1)
                if has(-1):
                    h_split(before, 2)
                if has(0):
                    probT_out(base, 2)
                    sums_inverse(base, 3)
                    oT_low(base, 2)
                if has(-1):
                    h_split(before, 3)
                if has(1):
                    edges(ahead)
                if has(0):
                    residual(base, 2)
                    ln2_stats(base, 2)
                if has(1):
                    edges_end(ahead)
                if has(0):
                    ln2_apply(base, 2)

            pipeline(dve, body)


_COLS = ['L0_gnn_' + n for n in ('ln1_g', 'ln1_b', 'ln2_g', 'ln2_b', 'bq', 'bk', 'bv', 'b1')]
_ROWS = ['L0_gnn_' + n for n in ('bo', 'b2')]
_INS = ['x', 'adj', 'vec_cols', 'vec_rows'] + ['L0_gnn_' + n for n in ('wq', 'wk', 'wv', 'wo', 'w1', 'w2')]
_OUTS = [((64, 128, 256), 'float32')]


def kernel(**inputs):
    import numpy as _np
    import concourse.bacc as _bacc
    from concourse import mybir as _mybir
    from concourse.bass_utils import run_bass_kernel_spmd as _run

    nc = _bacc.Bacc("TRN2", target_bir_lowering=False, num_devices=1)
    inputs = dict(inputs)
    inputs['vec_cols'] = _np.concatenate([inputs[n].reshape(-1, P).T for n in _COLS], axis=1)
    inputs['vec_rows'] = _np.concatenate([inputs[n] for n in _ROWS])
    arrays, args = {}, []
    for name in _INS:
        a = _np.ascontiguousarray(inputs[name])
        arrays[f"in_{name}_dram"] = a
        args.append(nc.dram_tensor(f"in_{name}_dram", a.shape, _mybir.dt.from_np(a.dtype), kind="ExternalInput").ap())
    for i, (shape, dtype) in enumerate(_OUTS):
        dt = _mybir.dt.from_np(_np.dtype(dtype))
        args.append(nc.dram_tensor(f"out_{i}_dram", shape, dt, kind="ExternalOutput").ap())
    gnn_layer(nc, *args)
    r = _run(nc, [arrays], core_ids=[0])
    got = tuple(r.results[0][f"out_{i}_dram"] for i in range(len(_OUTS)))
    return got[0]
```
